# Optimizing a Trainium2 kernel written in Bass

```python
import numpy as np
import jax
import jax.numpy as jnp

def _softmax(x, axis=-1):
    return jax.nn.softmax(x, axis=axis)

def _gelu(x):
    return jax.nn.gelu(x, approximate=True)

def _silu(x):
    return jax.nn.silu(x)

def _sigmoid(x):
    return jax.nn.sigmoid(x)

def _layernorm(x, axis=-1, eps=1e-05):
    m = jnp.mean(x, axis=axis, keepdims=True)
    v = jnp.var(x, axis=axis, keepdims=True)
    return (x - m) / jnp.sqrt(v + eps)

def _scatter_add(tgt, idx, src, axis=0):
    return tgt.at[idx].add(src)

def _segment_sum(src, seg, n):
    return jax.ops.segment_sum(src, seg, n)
kernel_name = 'mk_macaron_d1_jaxref_r8_150ebf'

def setup_inputs(seed: int=0):
    np.random.seed(seed)
    _w = jnp.asarray

    def _L0_attn_setup():
        import jax, jax.numpy as jnp
        import numpy as np
        B, S, E = (2, 512, 128)
        H = 16
        W = 32

        def _chunk3(x):
            prev = jnp.pad(x[:, :-1], ((0, 0), (1, 0), (0, 0), (0, 0), (0, 0)))
            nxt = jnp.pad(x[:, 1:], ((0, 0), (0, 1), (0, 0), (0, 0), (0, 0)))
            return jnp.stack([prev, x, nxt], axis=-1)
        key = jax.random.key(seed)
        ks = jax.random.split(key, 4)
        hs = jax.random.normal(ks[0], (B, S, E), jnp.float32)

        def lin(k):
            kw, kb = jax.random.split(k)
            return (jax.random.normal(kw, (E, E), jnp.float32) * 0.02, jax.random.normal(kb, (E,), jnp.float32) * 0.02)
        Wq, bq = lin(ks[1])
        Wk, bk = lin(ks[2])
        Wv, bv = lin(ks[3])
        return {'hidden_states': hs, 'Wq': Wq, 'bq': bq, 'Wk': Wk, 'bk': bk, 'Wv': Wv, 'bv': bv}
    _L0_attn_in = _L0_attn_setup()

    def _L0_ffn_setup():
        import jax, jax.numpy as jnp
        import numpy as np
        D_MODEL = 128
        N_EXPERTS = 8
        TOP_K = 2
        HIDDEN = 4 * D_MODEL
        key = jax.random.key(seed)
        ks = jax.random.split(key, 6)
        B, S = (2, 256)
        x = jax.random.normal(ks[0], (B, S, D_MODEL), dtype=jnp.float32)
        shared_w1 = jax.random.normal(ks[1], (HIDDEN, D_MODEL), dtype=jnp.float32) * 0.02
        shared_w2 = jax.random.normal(ks[2], (D_MODEL, HIDDEN), dtype=jnp.float32) * 0.02
        experts_w1 = jax.random.normal(ks[3], (N_EXPERTS, HIDDEN, D_MODEL), dtype=jnp.float32) * 0.02
        experts_w2 = jax.random.normal(ks[4], (N_EXPERTS, D_MODEL, HIDDEN), dtype=jnp.float32) * 0.02
        gate_w = jax.random.normal(ks[5], (N_EXPERTS, D_MODEL), dtype=jnp.float32) * 0.02
        return {'x': x, 'shared_w1': shared_w1, 'shared_w2': shared_w2, 'experts_w1': experts_w1, 'experts_w2': experts_w2, 'gate_w': gate_w}
    _L0_ffn_in = _L0_ffn_setup()
    _d = {'L0_attn_hidden_states': _L0_attn_in['hidden_states'], 'L0_attn_Wq': _L0_attn_in['Wq'], 'L0_attn_bq': _L0_attn_in['bq'], 'L0_attn_Wk': _L0_attn_in['Wk'], 'L0_attn_bk': _L0_attn_in['bk'], 'L0_attn_Wv': _L0_attn_in['Wv'], 'L0_attn_bv': _L0_attn_in['bv'], 'L0_ffn_shared_w1': _L0_ffn_in['shared_w1'], 'L0_ffn_shared_w2': _L0_ffn_in['shared_w2'], 'L0_ffn_experts_w1': _L0_ffn_in['experts_w1'], 'L0_ffn_experts_w2': _L0_ffn_in['experts_w2'], 'L0_ffn_gate_w': _L0_ffn_in['gate_w']}
    _x0 = _d['L0_attn_hidden_states']
    _d['L0_attn_hidden_states'] = jax.random.normal(jax.random.fold_in(jax.random.key(seed), 1), (2, 1024, 128), dtype=_x0.dtype)
    del _x0
    return _d

def reference(L0_attn_hidden_states, L0_attn_Wq, L0_attn_bq, L0_attn_Wk, L0_attn_bk, L0_attn_Wv, L0_attn_bv, L0_ffn_shared_w1, L0_ffn_shared_w2, L0_ffn_experts_w1, L0_ffn_experts_w2, L0_ffn_gate_w):

    def _L0_attn_ref(hidden_states, Wq, bq, Wk, bk, Wv, bv):
        import jax, jax.numpy as jnp
        import numpy as np
        B, S, E = (2, 512, 128)
        H = 16
        W = 32

        def _chunk3(x):
            prev = jnp.pad(x[:, :-1], ((0, 0), (1, 0), (0, 0), (0, 0), (0, 0)))
            nxt = jnp.pad(x[:, 1:], ((0, 0), (0, 1), (0, 0), (0, 0), (0, 0)))
            return jnp.stack([prev, x, nxt], axis=-1)
        b, s, e = hidden_states.shape
        h, w = (H, W)
        d = e // h
        nc = s // w
        q = (hidden_states @ Wq.T + bq) * (1.0 / np.sqrt(d))
        k = hidden_states @ Wk.T + bk
        v = hidden_states @ Wv.T + bv
        q = q.reshape(b, s, h, d)
        k = k.reshape(b, s, h, d)
        v = v.reshape(b, s, h, d)
        cq = q.reshape(b, nc, w, h, d)
        ck3 = _chunk3(k.reshape(b, nc, w, h, d))
        scores = jnp.einsum('bcxhd,bcyhde->bcxhey', cq, ck3).reshape(b, s, h, 3 * w)
        ii = jnp.arange(w)[:, None]
        cc = jnp.arange(w + 1)[None, :]
        beg_mask = cc < w - ii
        end_mask = cc >= w - ii
        neg_inf = jnp.array(-jnp.inf, scores.dtype)
        beg = jnp.where(beg_mask[None, :, None, :], neg_inf, scores[:, :w, :, :w + 1])
        scores = scores.at[:, :w, :, :w + 1].set(beg)
        end = jnp.where(end_mask[None, :, None, :], neg_inf, scores[:, s - w:, :, 3 * w - (w + 1):])
        scores = scores.at[:, s - w:, :, 3 * w - (w + 1):].set(end)
        probs = jax.nn.softmax(scores.astype(jnp.float32), axis=-1).astype(hidden_states.dtype)
        cp = probs.reshape(b, nc, w, h, 3, w)
        cv3 = _chunk3(v.reshape(b, nc, w, h, d))
        attn = jnp.einsum('bcwhpd,bcdhep->bcwhe', cp, cv3).reshape(b, s, h, d)
        return attn.reshape(b, s, e)

    def _L0_ffn_ref(x, shared_w1, shared_w2, experts_w1, experts_w2, gate_w):
        import jax, jax.numpy as jnp
        import numpy as np
        D_MODEL = 128
        N_EXPERTS = 8
        TOP_K = 2
        HIDDEN = 4 * D_MODEL
        B, S, D = x.shape
        T = B * S
        x_flat = x.reshape(T, D)
        shared = jnp.einsum('td,dh->th', x_flat, shared_w1.T)
        shared = jnp.einsum('th,hd->td', jax.nn.silu(shared), shared_w2.T)
        gate_logits = x_flat @ gate_w.T
        top_k_gates, top_k_idx = jax.lax.top_k(gate_logits, TOP_K)
        top_k_gates = jax.nn.softmax(top_k_gates, axis=1)
        gates = jnp.zeros((T, N_EXPERTS), dtype=x.dtype)
        gates = gates.at[jnp.arange(T)[:, None], top_k_idx].set(top_k_gates)
        h = jnp.einsum('td,ehd->teh', x_flat, experts_w1)
        expert_out = jnp.einsum('teh,edh->ted', jax.nn.silu(h), experts_w2)
        selected = jnp.einsum('ted,te->td', expert_out, gates)
        return (shared + selected).reshape(B, S, D)
    x = L0_attn_hidden_states
    x = x + 0.5 * _L0_ffn_ref(_layernorm(x, axis=-1), L0_ffn_shared_w1, L0_ffn_shared_w2, L0_ffn_experts_w1, L0_ffn_experts_w2, L0_ffn_gate_w)
    x = x + _L0_attn_ref(_layernorm(x, axis=-1), L0_attn_Wq, L0_attn_bq, L0_attn_Wk, L0_attn_bk, L0_attn_Wv, L0_attn_bv)
    x = x + 0.5 * _L0_ffn_ref(_layernorm(x, axis=-1), L0_ffn_shared_w1, L0_ffn_shared_w2, L0_ffn_experts_w1, L0_ffn_experts_w2, L0_ffn_gate_w)
    return x

_drawn_inputs = setup_inputs


def setup_inputs(seed=0):
    import zlib

    import numpy as np

    out = dict(_drawn_inputs(seed))
    spreads = {}
    factors = {'L0_attn_Wq': 8.0,
     'L0_attn_bq': 26.34,
     'L0_attn_Wk': 8.0,
     'L0_attn_bk': 64.0,
     'L0_attn_bv': 2.703}
    for name, (base, spread) in spreads.items():
        noise = np.random.default_rng([zlib.crc32(name.encode()), seed]).standard_normal(out[name].shape)
        drawn = base * np.exp(spread * noise) if base else spread * noise
        out[name] = jnp.asarray(drawn.astype(out[name].dtype))
    for name, factor in factors.items():
        out[name] = (out[name] * factor).astype(out[name].dtype)
    return out
```

```python
import numpy as np
import concourse.bass as bass
from concourse import mybir
from contextlib import ExitStack

P = 128
B, S, D = 2, 1024, 128
HID, NEXP = 512, 8
SHARED = NEXP
TILES = S // P
KCH = HID // P
SLOT_TILES = (2 * S + NEXP * (P - 1)) // P
UNITS = TILES + SLOT_TILES
HEADS, HD, W = 16, 8, 32
CHUNKS = S // W
CPB = P // W
HG = 4
KEYS = 3 * W
VG = W + 1
EPS = 1e-5
MASKED = -1.0e30

_WIDTHS = [("ident", P), ("tri", P), ("ones", P), ("sel", W), ("rep", P), ("beg", KEYS), ("end", KEYS),
           ("qmask", HG), ("gmask", HG), ("dmask", HG), ("rank", NEXP), ("cum", NEXP * NEXP), ("tile_no", SLOT_TILES),
           ("neg_half", TILES)]
CONST = {}
_at = 0
for _name, _w in _WIDTHS:
    CONST[_name] = (_at, _at + _w)
    _at += _w
NCONST = _at


def shape_constants():
    c = np.zeros((P, NCONST), np.float32)
    p = np.arange(P)

    def put(name, a):
        lo, hi = CONST[name]
        c[:, lo:hi] = np.asarray(a, np.float32).reshape(-1, hi - lo)

    put("ident", np.eye(P))
    put("tri", p[:, None] < p[None, :])
    put("ones", np.ones((P, P)))
    put("sel", (p[:, None] // HG) == np.arange(W)[None, :])
    put("rep", p[:, None] == (p[None, :] // HG))
    row, key = p[:, None] % W, np.arange(KEYS)[None, :]
    put("beg", np.where((key <= W) & (key < W - row), MASKED, 0.0))
    put("end", np.where((key >= 2 * W - 1) & (key - (2 * W - 1) >= W - row), MASKED, 0.0))
    inner = (p[:, None] % W) // HD == np.arange(HG)[None, :]
    put("qmask", inner * np.float32(1.0 / np.sqrt(HD)))
    put("gmask", p[:, None] // W == np.arange(HG)[None, :])
    put("dmask", p[:, None] % HG == np.arange(HG)[None, :])
    put("rank", np.tile(NEXP - np.arange(NEXP), (P, 1)))
    put("cum", np.tile((np.arange(NEXP)[None, :] <= np.arange(NEXP)[:, None]).ravel(), (P, 1)))
    put("tile_no", np.tile(np.arange(SLOT_TILES), (P, 1)))
    put("neg_half", np.full((P, TILES), -0.5))
    return c


def macaron_kernel(nc, x_in, consts, w1t, w2t, gate_wt, wqt, wkt, wvt, bqk, bv_rows, out):
    f32, i32 = mybir.dt.float32, mybir.dt.int32
    ALU, ACT, AX = mybir.AluOpType, mybir.ActivationFunctionType, mybir.AxisListType

    ctx = ExitStack()
    with ctx:
        def sb(name, shape, dt=f32):
            return ctx.enter_context(nc.sbuf_tensor(name, shape, dt))

        def sem(name):
            return ctx.enter_context(nc.semaphore(name))

        normed = [nc.dram_tensor(f"normed{b}", (S, D), f32).ap() for b in range(B)]
        rows = [nc.dram_tensor(f"expert_rows{b}", (SLOT_TILES * P, D), f32).ap() for b in range(B)]
        yrows = [nc.dram_tensor(f"expert_out{b}", (SLOT_TILES * P, D), f32).ap() for b in range(B)]
        vpad = [nc.dram_tensor(f"v_padded{b}", (S + 2 * W, HG * VG), f32).ap() for b in range(B)]

        cst = sb("cst", [P, NCONST])

        def const(name):
            lo, hi = CONST[name]
            return cst[:, lo:hi]

        ident, tri, ones, sel, rep = (const(n) for n in ("ident", "tri", "ones", "sel", "rep"))
        x = sb("x", [P, B, TILES, D])
        xn = sb("xn", [P, B, TILES, D])
        xnt = sb("xnt", [P, B, TILES * P])
        w1 = sb("w1", [P, NEXP + 1, HID])
        w2 = sb("w2", [P, NEXP + 1, KCH, D])
        gw = sb("gw", [P, NEXP])
        wq, wk, wv = sb("wq", [P, D]), sb("wk", [P, D]), sb("wv", [P, D])
        bias = sb("bias", [P, 2])
        bv = sb("bv", [P, D])
        zero = sb("zero", [P, SLOT_TILES * D])

        stats = sb("stats", [P, TILES, 6])
        mv = sb("mv", [P, TILES, 2])
        vare = sb("vare", [P, TILES])
        rstd = sb("rstd", [P, TILES])

        logit = sb("logit", [P, TILES, NEXP])
        top = sb("top", [P, 2, TILES])
        hit = sb("hit", [P, TILES, NEXP])
        best = sb("best", [P, TILES])
        onehot = sb("onehot", [P, 2, TILES, NEXP])
        chosen = sb("chosen", [P, TILES + 1, NEXP])
        gap, egap = sb("gap", [P, TILES]), sb("egap", [P, TILES])
        rden = sb("rden", [P, TILES])
        gate = sb("gate", [P, B, 2, TILES])
        count = sb("count", [P, NEXP], i32)
        ntile = sb("ntile", [P, NEXP])
        ends8 = sb("ends8", [P, NEXP, NEXP])
        end_tile = sb("end_tile", [P, NEXP])
        base = sb("base", [P, NEXP])
        slot = sb("slot", [P, TILES, NEXP])
        slot2 = sb("slot2", [P, 2, TILES, NEXP])
        slotf = sb("slotf", [P, 2, TILES])
        slot_i = sb("slot_i", [P, B, 2, TILES], i32)
        passed = sb("passed", [1, SLOT_TILES, NEXP])
        tile_ef = sb("tile_ef", [1, SLOT_TILES])
        tile_e = sb("tile_e", [1, B, UNITS], i32)

        xrow = sb("xrow", [P, 4, D])
        xt = sb("xt", [P, 2, P])
        th = sb("th", [P, 2, HID])
        act = sb("act", [P, 2, HID])
        act_t = sb("act_t", [P, 2, KCH * P])
        yall = sb("yall", [P, B, UNITS, D])
        got = sb("got", [P, B, 2, TILES, D])

        kt = sb("kt", [P, HG, S + 2 * W])
        bkg = sb("bkg", [P, HG])
        vsb = sb("vsb", [P, TILES, HG, VG])
        vend = sb("vend", [W, HG, VG])
        vwin = sb("vwin", [KEYS, CHUNKS, HG * VG])
        qbd = sb("qbd", [P, 2, P * HG])
        mx = sb("mx", [P, 2, CPB])
        cen = sb("cen", [P, 2, CPB, KEYS])
        prob = sb("prob", [P, 2, CPB, KEYS])
        prob_t = sb("prob_t", [KEYS, 2, CPB * P])
        rsum = sb("rsum", [P, HG * CPB])
        rmask = sb("rmask", [P, HG * CPB, HG])
        omix = sb("omix", [P, HG * CPB, W])

        ps = ctx.enter_context(nc.psum_tensor("ps", [P, 8, 512], f32))
        misc = [6, 7]

        const_in, x_in_sem, w_in, qkv_in, zeroed = (sem(n) for n in ("const_in", "x_arrived", "w_in", "qkv_in", "zeroed"))
        zero_set, preset = sem("zero_set"), sem("preset")
        dve_step = sem("dve_step")
        vare_ready, rstd_ready, xn_ready = sem("vare_ready"), sem("rstd_ready"), sem("xn_ready")
        half_turned, half_copied = sem("half_turned"), sem("half_copied")
        logits_ready, chosen_ready, pos_ready = sem("logits_ready"), sem("chosen_ready"), sem("pos_ready")
        gap_ready, egap_ready, route_ready = sem("gap_ready"), sem("egap_ready"), sem("route_ready")
        xn_stored, scattered = ([sem(f"{n}{b}") for b in range(B)] for n in ("xn_stored", "scattered"))
        row_in = [sem(f"row_in{i}") for i in range(4)]
        xt_turned, xt_ready, h_ready, th_ready, act_ready = (sem(n) for n in ("xt_turned", "xt_ready", "h_ready", "th_ready", "act_ready"))
        act_turned, act_t_ready, y_ready, y_copied = (sem(n) for n in ("act_turned", "act_t_ready", "y_ready", "y_copied"))
        y_stored = [sem(f"y_stored{b}") for b in range(B)]
        gathered = [sem(f"gathered{b}") for b in range(B)]
        k_proj, k_ready, v_proj, v_ready, v_stored, vwin_in = (sem(n) for n in ("k_proj", "k_ready", "v_proj", "v_ready", "v_stored", "vwin_in"))
        q_proj, q_ready, s_ready, mx_ready, cen_ready, prob_ready = (sem(n) for n in ("q_proj", "q_ready", "s_ready", "mx_ready", "cen_ready", "prob_ready"))
        prob_turned, prob_t_ready, o_ready, omix_ready, sel_ready, x2_ready = (sem(n) for n in ("prob_turned", "prob_t_ready", "o_ready", "omix_ready", "sel_ready", "x2_ready"))
        rsum_ready, rmask_ready = sem("rsum_ready"), sem("rmask_ready")
        bkg_ready = sem("bkg_ready")
        x_done, stored = sem("x_done"), sem("stored")

        STAGES = [("route", 0, 0), ("route", 0, 1), ("units", 0, 0), ("units", 0, 1),
                  ("attn", 0, 0), ("route", 1, 0), ("attn", 0, 1), ("route", 1, 1),
                  ("units", 1, 0), ("units", 1, 1), ("last", 1, 0), ("last", 1, 1)]
        ln_no = {s: n for n, s in enumerate([s for s in STAGES if s[0] in ("route", "attn")])}

        def fb(f, b):
            return f * B + b

        Y_STORES = (UNITS - 12) // 4 + 1

        block = ctx.enter_context(nc.Block())

        @block.sync
        def _(sp):
            sp.dma_start(x[:, 0], x_in[0].rearrange("(t p) d -> p t d", p=P)).then_inc(x_in_sem, 16)
            sp.dma_start(cst[:, :], consts).then_inc(const_in, 16)
            sp.dma_start(gw[:, :], gate_wt).then_inc(const_in, 16)
            sp.wait_ge(x_in_sem, 16)
            sp.dma_start(x[:, 1], x_in[1].rearrange("(t p) d -> p t d", p=P)).then_inc(x_in_sem, 16)
            sp.dma_start(w1[:, SHARED], w1t[:, SHARED]).then_inc(w_in, 16)
            sp.dma_start(w2[:, SHARED], w2t[:, SHARED]).then_inc(w_in, 16)
            sp.dma_start(w1[:, 0:NEXP], w1t[:, 0:NEXP]).then_inc(w_in, 16)
            sp.dma_start(w2[:, 0:NEXP], w2t[:, 0:NEXP]).then_inc(w_in, 16)
            for dst, src in ((wq, wqt), (wk, wkt), (wv, wvt), (bias, bqk), (bv, bv_rows)):
                sp.dma_start(dst[:, :], src).then_inc(qkv_in, 16)

            def units(f, b):
                g0 = fb(f, b) * UNITS
                sp.wait_ge(xn_stored[b], 16 * (f + 1))

                def load(u, k):
                    if not isinstance(u, int) or g0 + u >= 4:
                        sp.wait_ge(xt_turned, u + (g0 - 3))
                    if isinstance(u, int) and u < TILES:
                        src = normed[b][u * P:(u + 1) * P, :]
                    else:
                        src = rows[b][bass.ds((u - TILES) * P, P), :]
                    sp.dma_start(xrow[:, k], src).then_inc(row_in[k], 16)

                for k in range(4):
                    load(k, k)
                for k in range(4):
                    load(4 + k, k)
                sp.wait_ge(scattered[b], 16 * 2 * TILES * (f + 1))
                for k in range(4):
                    load(8 + k, k)
                full = (UNITS - 12) // 4
                with sp.Fori(12, 12 + 4 * full - 3, 4) as u:
                    for k in range(4):
                        load(u + k, k)
                    sp.wait_ge(y_copied, u + (g0 + 4 - 4))
                    sp.dma_start(yrows[b][bass.ds((u - (4 + TILES)) * P, 4 * P), :].rearrange("(t p) d -> p t d", p=P),
                                 yall[:, b, bass.ds(u - 4, 4), :]).then_inc(y_stored[b], 16)
                for u in range(12 + 4 * full, UNITS):
                    load(u, u % 4)
                first = 12 + 4 * full - 4
                sp.wait_ge(y_copied, g0 + UNITS)
                sp.dma_start(yrows[b][(first - TILES) * P:, :].rearrange("(t p) d -> p t d", p=P),
                             yall[:, b, first:, :]).then_inc(y_stored[b], 16)

            def xn_store(f, b):
                sp.wait_ge(xn_ready, ln_no[("route", f, b)] + 1)
                if f:
                    sp.wait_ge(xt_turned, (b + 1) * UNITS)
                sp.dma_start(normed[b].rearrange("(t p) d -> p t d", p=P), xn[:, b]).then_inc(xn_stored[b], 16)

            def attn(b):
                if b == 0:
                    sp.wait_ge(preset, 3)
                    for bb in range(B):
                        for at in (0, S + W):
                            sp.dma_start(vpad[bb][at:at + W, :], vend[:, :, :].rearrange("p g n -> p (g n)")).then_inc(v_stored, 16)
                sp.wait_ge(v_ready, 2 * (b + 1))
                sp.dma_start(vpad[b][W:W + S, :].rearrange("(t p) n -> p t n", p=P),
                             vsb[:, :, :, :].rearrange("p t g n -> p t (g n)")).then_inc(v_stored, 16)
                sp.wait_ge(v_stored, 16 * (5 + b))
                for part in range(3):
                    sp.dma_start(vwin[part * W:(part + 1) * W, :, :],
                                 vpad[b][part * W:part * W + S, :].rearrange("(c p) n -> p c n", p=W)).then_inc(vwin_in, 16)

            def last(b):
                sp.wait_ge(x_done, b + 1)
                sp.dma_start(out[b].rearrange("(t p) d -> p t d", p=P), x[:, b]).then_inc(stored, 16)

            for kind, f, b in STAGES:
                if kind == "units":
                    units(f, b)
                elif kind == "route":
                    xn_store(f, b)
                elif kind == "attn":
                    attn(b)
                else:
                    last(b)
            sp.wait_ge(stored, 16 * B)

        @block.gpsimd
        def _(pool):
            pool.memset(zero[:, :], 0.0).then_inc(zero_set, 1)
            pool.memset(chosen[:, TILES, :], 0.0).then_inc(preset, 1)
            pool.memset(vend[:, :, 0:W], 0.0).then_inc(preset, 1)
            pool.memset(vend[:, :, W:VG], 1.0).then_inc(preset, 1)
            pool.memset(vsb[:, :, :, W:VG], 1.0).then_inc(preset, 1)
            pool.memset(kt[:, :, 0:W], 0.0).then_inc(preset, 1)
            pool.memset(kt[:, :, W + S:], 0.0).then_inc(preset, 1)
            pool.memset(tile_e[:, :, 0:TILES], SHARED).then_inc(preset, 1)

            def norm(n):
                pool.wait_ge(vare_ready, n + 1)
                if n == 0:
                    pool.wait_ge(const_in, 32)
                pool.tensor_tensor(rstd[:, :], vare[:, :], const("neg_half"), ALU.pow).then_inc(rstd_ready, 1)

            def scatter(f, b):
                pool.wait_ge(route_ready, fb(f, b) + 1)
                if fb(f, b) < B:
                    pool.wait_ge(zeroed, 16 * B)
                for t in range(TILES):
                    for k in range(2):
                        pool.indirect_dma_start(
                            out=rows[b], out_offset=bass.IndirectOffsetOnAxis(ap=slot_i[:, b, k, t:t + 1], axis=0),
                            in_=xn[:, b, t, :], in_offset=None).then_inc(scattered[b], 16)

            def gather(f, b):
                pool.wait_ge(y_stored[b], 16 * Y_STORES * (f + 1))
                for t in range(TILES):
                    for k in range(2):
                        pool.indirect_dma_start(
                            out=got[:, b, k, t, :], out_offset=None, in_=yrows[b],
                            in_offset=bass.IndirectOffsetOnAxis(ap=slot_i[:, b, k, t:t + 1], axis=0)).then_inc(gathered[b], 16)

            for kind, f, b in STAGES:
                if kind == "route":
                    norm(ln_no[(kind, f, b)])
                    scatter(f, b)
                elif kind == "units":
                    gather(f, b)
                elif kind == "attn":
                    norm(ln_no[(kind, f, b)])

        @block.scalar
        def _(s):
            s.wait_ge(zero_set, 1)
            for b in range(B):
                s.dma_start(rows[b].rearrange("(t p) d -> p t d", p=P),
                            zero[:, :].rearrange("p (t d) -> p t d", d=D)).then_inc(zeroed, 16)

            def copy_halves(n, b):
                for h in range(2):
                    s.wait_ge(half_turned, 2 * n + h + 1)
                    s.activation(xnt[:, b, h * 512:(h + 1) * 512], ps[:, misc[h], :], ACT.Copy).then_inc(half_copied, 1)

            def route(f, b):
                copy_halves(ln_no[("route", f, b)], b)
                s.wait_ge(gap_ready, fb(f, b) + 1)
                s.activation(egap[:, :], gap[:, :], ACT.Exp).then_inc(egap_ready, 1)

            def units(f, b):
                g0 = fb(f, b) * UNITS

                def tanh(u, k):
                    s.wait_ge(h_ready, u + (g0 + 1))
                    if not isinstance(u, int) or u >= 2:
                        s.wait_ge(act_ready, u + (g0 - 1))
                    elif g0:
                        s.wait_ge(act_ready, g0)
                    s.activation(th[:, k, :], ps[:, k, :], ACT.Tanh, scale=0.5).then_inc(th_ready, 1)

                def copy_act(u, k):
                    s.wait_ge(act_turned, u + (g0 + 1))
                    if not isinstance(u, int) or u >= 2:
                        s.wait_ge(y_ready, u + (g0 - 1))
                    elif g0:
                        s.wait_ge(y_ready, g0)
                    s.activation(act_t[:, k, :], ps[:, 2, :], ACT.Copy, scale=0.5).then_inc(act_t_ready, 1)

                tanh(0, 0)
                for u in range(1, 3):
                    tanh(u, u % 2)
                    copy_act(u - 1, (u - 1) % 2)
                with s.Fori(3, UNITS - 1, 2) as u:
                    for j in range(2):
                        tanh(u + j, (3 + j) % 2)
                        copy_act(u + (j - 1), j % 2)
                copy_act(UNITS - 1, (UNITS - 1) % 2)

            def attn(b):
                n = ln_no[("attn", 0, b)]
                copy_halves(n, b)
                if b == 0:
                    s.wait_ge(preset, 7)
                    s.wait_ge(bkg_ready, 1)
                for h in range(2):
                    s.wait_ge(k_proj, 2 * b + h + 1)
                    for g in range(HG):
                        last = s.activation(kt[:, g, W + h * 512:W + (h + 1) * 512], ps[:, misc[h], :], ACT.Identity,
                                            bias=bkg[:, g:g + 1], scale=const("gmask")[:, g:g + 1])
                    last.then_inc(k_ready, 1)
                v0 = b * TILES * HG

                def exp(v, k):
                    s.wait_ge(cen_ready, v + (v0 + 1))
                    if not isinstance(v, int) or v0 + v >= 2:
                        s.wait_ge(prob_turned, v + (v0 - 1))
                    s.activation(prob[:, k], cen[:, k], ACT.Exp).then_inc(prob_ready, 1)

                def copy_prob(v, k):
                    s.wait_ge(prob_turned, v + (v0 + 1))
                    if not isinstance(v, int) or v0 + v >= 2:
                        s.wait_ge(o_ready, v + (v0 - 1))
                    s.activation(prob_t[:, k, :], ps[0:KEYS, 2 + k, :], ACT.Copy).then_inc(prob_t_ready, 1)

                exp(0, 0)
                exp(1, 1)
                copy_prob(0, 0)
                with s.Fori(2, TILES * HG - 1, 2) as v:
                    for j in range(2):
                        exp(v + j, j)
                        copy_prob(v + (j - 1), 1 - j)
                copy_prob(TILES * HG - 1, 1)

            for kind, f, b in STAGES:
                if kind == "route":
                    route(f, b)
                elif kind == "units":
                    units(f, b)
                elif kind == "attn":
                    attn(b)

        @block.tensor
        def _(pe):
            pe.wait_ge(const_in, 32)

            def turn_halves(n, b):
                pe.wait_ge(xn_ready, n + 1)
                for h in range(2):
                    for t in range(4):
                        last = pe.transpose(ps[:, misc[h], t * P:(t + 1) * P], xn[:, b, 4 * h + t, :], ident)
                    last.then_inc(half_turned, 1)

            def route(f, b):
                n, r = ln_no[("route", f, b)], fb(f, b)
                turn_halves(n, b)
                pe.wait_ge(half_copied, 2 * n + 2)
                for t in range(TILES):
                    last = pe.matmul(ps[:, misc[0], t * NEXP:(t + 1) * NEXP], xnt[:, b, t * P:(t + 1) * P], gw[:, :],
                                     start=True, stop=True)
                last.then_inc(logits_ready, 1)
                pe.wait_ge(chosen_ready, r + 1)
                for t in range(TILES):
                    pe.matmul(ps[:, misc[1], (t + 1) * NEXP:(TILES + 1) * NEXP].rearrange("p (t e) -> p t e", e=NEXP),
                              ones, chosen[:, t:t + 1, :].to_broadcast([P, TILES - t, NEXP]),
                              start=(t == 0), stop=False, skip_group_check=True)
                last = pe.matmul(ps[:, misc[1], 0:(TILES + 1) * NEXP], tri, chosen[:, :, :].rearrange("p t e -> p (t e)"),
                                 start=False, stop=True, skip_group_check=True)
                last.then_inc(pos_ready, 1)

            def units(f, b):
                r = fb(f, b)
                g0 = r * UNITS
                pe.wait_ge(route_ready, r + 1)
                if r == 0:
                    pe.wait_ge(w_in, 16 * 4)
                if f == 1 and b == 0:
                    pe.wait_ge(x2_ready, B * TILES)
                if g0:
                    pe.wait_ge(act_ready, g0)
                    pe.wait_ge(act_t_ready, g0)
                    pe.wait_ge(y_copied, g0)
                arrived = [r * len(range(k, UNITS, 4)) for k in range(4)]

                def turn_rows(u, k):
                    if isinstance(u, int):
                        pe.wait_ge(row_in[k], 16 * (arrived[k] + u // 4 + 1))
                    else:
                        pe.wait_ge(row_in[k], (u + (4 * (arrived[k] + 1) - k)) * 4)
                    pe.wait_ge(xt_ready, u + g0)
                    pe.transpose(ps[:, 4, 0:P], xrow[:, k, :], ident).then_inc(xt_turned, 1)

                def up(u, k):
                    e = pe.value_load(tile_e[0:1, b, bass.ds(u, 1)], min_val=0, max_val=NEXP)
                    pe.wait_ge(xt_ready, u + (g0 + 1))
                    if not isinstance(u, int) or u >= 2:
                        pe.wait_ge(act_ready, u + (g0 - 1))
                    pe.matmul(ps[:, k, :], xt[:, k, :], w1[:, bass.ds(e, 1), :].rearrange("p a n -> p (a n)"),
                              start=True, stop=True).then_inc(h_ready, 1)

                def turn_act(u, k):
                    pe.wait_ge(act_ready, u + (g0 + 1))
                    pe.wait_ge(act_t_ready, u + g0)
                    for c in range(KCH):
                        last = pe.transpose(ps[:, 2, c * P:(c + 1) * P], act[:, k, c * P:(c + 1) * P], ident)
                    last.then_inc(act_turned, 1)

                def down(u, k):
                    e = pe.value_load(tile_e[0:1, b, bass.ds(u, 1)], min_val=0, max_val=NEXP)
                    pe.wait_ge(act_t_ready, u + (g0 + 1))
                    pe.wait_ge(y_copied, u + g0)
                    for c in range(KCH):
                        last = pe.matmul(ps[:, 3, 0:D], act_t[:, k, c * P:(c + 1) * P],
                                         w2[:, bass.ds(e, 1), c, :].rearrange("p a n -> p (a n)"),
                                         start=(c == 0), stop=(c == KCH - 1))
                    last.then_inc(y_ready, 1)

                turn_rows(0, 0)
                for u in range(3):
                    turn_rows(u + 1, (u + 1) % 4)
                    up(u, u % 2)
                    if u >= 1:
                        turn_act(u - 1, (u - 1) % 2)
                    if u >= 2:
                        down(u - 2, (u - 2) % 2)
                loops = (UNITS - 4) // 4
                with pe.Fori(3, 4 * loops, 4) as u:
                    for j in range(4):
                        turn_rows(u + (j + 1), j)
                        up(u + j, (3 + j) % 2)
                        turn_act(u + (j - 1), (2 + j) % 2)
                        down(u + (j - 2), (1 + j) % 2)
                for u in range(3 + 4 * loops, UNITS):
                    if u + 1 < UNITS:
                        turn_rows(u + 1, (u + 1) % 4)
                    up(u, u % 2)
                    turn_act(u - 1, (u - 1) % 2)
                    down(u - 2, (u - 2) % 2)
                u = UNITS
                turn_act(u - 1, (u - 1) % 2)
                down(u - 2, (u - 2) % 2)
                down(u - 1, (u - 1) % 2)

            def attn(b):
                n = ln_no[("attn", 0, b)]
                turn_halves(n, b)
                pe.wait_ge(half_copied, 2 * n + 2)
                if b == 0:
                    pe.wait_ge(qkv_in, 16 * 5)
                for h in range(2):
                    pe.matmul(ps[:, misc[h], :], wk[:, :], xnt[:, b, h * 512:(h + 1) * 512],
                              start=True, stop=True).then_inc(k_proj, 1)
                for h in range(2):
                    pe.wait_ge(k_ready, 2 * b + h + 1)
                    for t in range(4):
                        last = pe.matmul(ps[:, misc[h], t * P:(t + 1) * P], xnt[:, b, (4 * h + t) * P:(4 * h + t + 1) * P],
                                         wv[:, :], start=True, stop=True)
                    last.then_inc(v_proj, 1)
                blk0, v0 = b * TILES, b * TILES * HG
                pe.wait_ge(v_ready, 2 * (b + 1))
                pe.wait_ge(vwin_in, 16 * 3 * (b + 1))
                pe.wait_ge(act_ready, B * UNITS)
                pe.wait_ge(act_t_ready, B * UNITS)
                pe.wait_ge(y_copied, B * UNITS)

                def q_block(blk):
                    pe.wait_ge(q_ready, blk + blk0)
                    pe.matmul(ps[:, 6, 0:P], wq[:, :], xnt[:, b, bass.ds(blk * P, P)], start=True, stop=True)\
                      .then_inc(q_proj, 1)

                def scores(blk, g, ring, edge):
                    v = blk * HG + g
                    if g == 0:
                        pe.wait_ge(q_ready, blk + (blk0 + 1))
                    if not isinstance(v, int) or v0 + v >= 2:
                        pe.wait_ge(cen_ready, v + (v0 - 1))
                    for c in range(CPB):
                        mask = "beg" if edge == 0 and c == 0 else "end" if edge == 1 and c == CPB - 1 else None
                        dst = ps[:, g % 2, c * KEYS:(c + 1) * KEYS]
                        last = pe.matmul(dst, qbd[:, ring, c * P:(c + 1) * P],
                                         kt[:, g, bass.ds(blk * P + c * W, KEYS)], start=True, stop=(mask is None))
                        if mask:
                            last = pe.matmul(dst, rep, const(mask), start=False, stop=True)
                    last.then_inc(s_ready, 1)

                def turn_prob(v, k):
                    pe.wait_ge(prob_ready, v + (v0 + 1))
                    if not isinstance(v, int) or v0 + v >= 2:
                        pe.wait_ge(prob_t_ready, v + (v0 - 1))
                    for c in range(CPB):
                        last = pe.transpose(ps[0:KEYS, 2 + k, c * P:(c + 1) * P], prob[:, k, c, :], ident)
                    last.then_inc(prob_turned, 1)

                def mix(blk, g):
                    v = blk * HG + g
                    pe.wait_ge(prob_t_ready, v + (v0 + 1))
                    if g == 0 and (not isinstance(blk, int) or blk0 + blk >= 1):
                        pe.wait_ge(omix_ready, (blk + blk0) * 2)
                    for c in range(CPB):
                        at = (g % 2) * CPB * VG + c * VG
                        last = pe.matmul(ps[:, 4 + g // 2, at:at + VG], prob_t[:, g % 2, c * P:(c + 1) * P],
                                         vwin[:, bass.ds(blk * CPB + c, 1), g * VG:(g + 1) * VG].rearrange("p a n -> p (a n)"),
                                         start=True, stop=True)
                    last.then_inc(o_ready, 1)

                def pick(blk):
                    pe.wait_ge(omix_ready, (blk + blk0) * 2 + 2)
                    if not isinstance(blk, int) or blk0 + blk >= 1:
                        pe.wait_ge(x2_ready, blk + blk0)
                    for c in range(CPB):
                        last = pe.matmul(ps[c * W:(c + 1) * W, 7, 0:D], sel,
                                         omix[:, :, :].rearrange("p (g c) n -> p g c n", c=CPB)[:, :, c, :],
                                         start=True, stop=True)
                    last.then_inc(sel_ready, 1)

                def unit(blk, g, ring, edge):
                    v = blk * HG + g
                    scores(blk, g, ring, edge)
                    if g == 1:
                        nxt = blk + 1
                        if not isinstance(blk, int) or blk + 1 < TILES:
                            q_block(nxt)
                    if not isinstance(v, int) or v >= 1:
                        turn_prob(v - 1, (g - 1) % 2)
                    if not isinstance(v, int) or v >= 2:
                        mix(blk if g >= 2 else blk - 1, (g - 2) % HG)
                    if g == 2 and (not isinstance(blk, int) or blk >= 1):
                        pick(blk - 1)

                q_block(0)
                for g in range(HG):
                    unit(0, g, 0, 0)
                with pe.Fori(1, TILES - 2, 2) as blk:
                    for j in range(2):
                        for g in range(HG):
                            unit(blk + j, g, (1 + j) % 2, None)
                end = TILES - 1
                for g in range(HG):
                    unit(end, g, end % 2, 1)
                turn_prob(TILES * HG - 1, 1)
                mix(end, 2)
                mix(end, 3)
                pick(end)

            for kind, f, b in STAGES:
                if kind == "route":
                    route(f, b)
                elif kind == "units":
                    units(f, b)
                elif kind == "attn":
                    attn(b)

        @block.vector
        def _(v):
            steps = [0]

            def step(ins):
                steps[0] += 1
                ins.then_inc(dve_step, 1)
                v.wait_ge(dve_step, steps[0])

            def norm(n, b):
                for t in range(TILES):
                    last = v.bn_stats(stats[:, t, :], x[:, b, t, :])
                step(last)
                for t in range(TILES):
                    last = v.bn_aggr(mv[:, t, :], stats[:, t, :])
                step(last)
                v.tensor_scalar(vare[:, :], mv[:, :, 1], EPS, None, ALU.add).then_inc(vare_ready, 1)
                v.wait_ge(rstd_ready, n + 1)
                for t in range(TILES):
                    last = v.tensor_scalar(xn[:, b, t, :], x[:, b, t, :], mv[:, t, 0:1], rstd[:, t:t + 1],
                                           ALU.subtract, ALU.mult)
                last.then_inc(xn_ready, 1)

            def over_experts(a):
                return a.unsqueeze(2).to_broadcast([P, TILES, NEXP])

            def route(f, b):
                n, r = ln_no[("route", f, b)], fb(f, b)
                if f == 0:
                    v.wait_ge(x_in_sem, 16 * (b + 1))
                norm(n, b)
                v.wait_ge(logits_ready, r + 1)
                if r == 0:
                    v.wait_ge(const_in, 32)
                    v.wait_ge(preset, 7)
                step(v.tensor_copy(logit[:, :, :], ps[:, misc[0], 0:TILES * NEXP].rearrange("p (t e) -> p t e", e=NEXP)))
                rank = const("rank").unsqueeze(1).to_broadcast([P, TILES, NEXP])
                for k in range(2):
                    step(v.tensor_reduce(top[:, k, :], logit[:, :, :], AX.X, ALU.max))
                    step(v.tensor_tensor(hit[:, :, :], logit[:, :, :], over_experts(top[:, k, :]), ALU.is_equal))
                    step(v.tensor_tensor(hit[:, :, :], hit[:, :, :], rank, ALU.mult))
                    step(v.tensor_reduce(best[:, :], hit[:, :, :], AX.X, ALU.max))
                    step(v.tensor_tensor(onehot[:, k], rank, over_experts(best[:, :]), ALU.is_equal))
                    if k == 0:
                        step(v.scalar_tensor_tensor(logit[:, :, :], onehot[:, 0], -3.0e38, logit[:, :, :], ALU.mult, ALU.add))
                v.tensor_tensor(chosen[:, 0:TILES, :], onehot[:, 0], onehot[:, 1], ALU.add).then_inc(chosen_ready, 1)
                v.tensor_tensor(gap[:, :], top[:, 1, :], top[:, 0, :], ALU.subtract).then_inc(gap_ready, 1)
                v.wait_ge(egap_ready, r + 1)
                step(v.tensor_scalar(rden[:, :], egap[:, :], 1.0, None, ALU.add))
                step(v.reciprocal(rden[:, :], rden[:, :]))
                step(v.tensor_scalar(gate[:, b, 0, :], rden[:, :], 0.5, None, ALU.mult))
                step(v.tensor_tensor(gate[:, b, 1, :], gate[:, b, 0, :], egap[:, :], ALU.mult))
                v.wait_ge(pos_ready, r + 1)
                pos = ps[:, misc[1], 0:TILES * NEXP].rearrange("p (t e) -> p t e", e=NEXP)
                cnt = ps[:, misc[1], TILES * NEXP:(TILES + 1) * NEXP]
                step(v.tensor_scalar(count[:, :], cnt, float(P - 1), None, ALU.add))
                step(v.tensor_scalar(count[:, :], count[:, :], 7, None, ALU.logical_shift_right))
                step(v.tensor_copy(ntile[:, :], count[:, :]))
                step(v.tensor_tensor(ends8[:, :, :], ntile[:, :].unsqueeze(1).to_broadcast([P, NEXP, NEXP]),
                                     const("cum").rearrange("p (a c) -> p a c", c=NEXP), ALU.mult))
                step(v.tensor_reduce(end_tile[:, :], ends8[:, :, :], AX.X, ALU.add))
                step(v.tensor_tensor(passed[:, :, :], end_tile[0:1, :].unsqueeze(1).to_broadcast([1, SLOT_TILES, NEXP]),
                                     const("tile_no")[0:1, :].unsqueeze(2).to_broadcast([1, SLOT_TILES, NEXP]), ALU.is_le))
                step(v.tensor_reduce(tile_ef[:, :], passed[:, :, :], AX.X, ALU.add))
                step(v.tensor_scalar(tile_e[:, b, TILES:UNITS], tile_ef[:, :], float(NEXP - 1), None, ALU.min))
                step(v.tensor_tensor(base[:, :], end_tile[:, :], ntile[:, :], ALU.subtract))
                step(v.tensor_scalar(base[:, :], base[:, :], float(P), None, ALU.mult))
                step(v.tensor_tensor(slot[:, :, :], pos, base[:, :].unsqueeze(1).to_broadcast([P, TILES, NEXP]), ALU.add))
                for k in range(2):
                    step(v.tensor_tensor(slot2[:, k], slot[:, :, :], onehot[:, k], ALU.mult))
                step(v.tensor_reduce(slotf[:, :, :], slot2[:, :, :, :], AX.X, ALU.add))
                v.tensor_copy(slot_i[:, b, :, :], slotf[:, :, :]).then_inc(route_ready, 1)

            def units(f, b):
                g0 = fb(f, b) * UNITS

                def copy_xt(u, k):
                    v.wait_ge(xt_turned, u + (g0 + 1))
                    if not isinstance(u, int) or u >= 2:
                        v.wait_ge(h_ready, u + (g0 - 1))
                    elif g0:
                        v.wait_ge(h_ready, g0)
                    v.tensor_copy(xt[:, k, :], ps[:, 4, 0:P]).then_inc(xt_ready, 1)

                def silu(u, k):
                    v.wait_ge(th_ready, u + (g0 + 1))
                    if not isinstance(u, int) or u >= 2:
                        v.wait_ge(act_turned, u + (g0 - 1))
                    elif g0:
                        v.wait_ge(act_turned, g0)
                    v.scalar_tensor_tensor(act[:, k, :], th[:, k, :], 1.0, ps[:, k, :], ALU.add, ALU.mult)\
                     .then_inc(act_ready, 1)

                def copy_y(u):
                    v.wait_ge(y_ready, u + (g0 + 1))
                    v.tensor_copy(yall[:, b, bass.ds(u, 1), :].rearrange("p a n -> p (a n)"), ps[:, 3, 0:D])\
                     .then_inc(y_copied, 1)

                if f:
                    v.wait_ge(y_stored[b], 16 * Y_STORES)
                copy_xt(0, 0)
                for u in range(3):
                    copy_xt(u + 1, (u + 1) % 2)
                    silu(u, u % 2)
                    if u >= 2:
                        copy_y(u - 2)
                with v.Fori(3, UNITS - 3, 2) as u:
                    for j in range(2):
                        copy_xt(u + (j + 1), j % 2)
                        silu(u + j, (3 + j) % 2)
                        copy_y(u + (j - 2))
                copy_xt(UNITS - 1, (UNITS - 1) % 2)
                for u in range(UNITS - 2, UNITS):
                    silu(u, u % 2)
                    copy_y(u - 2)
                copy_y(UNITS - 2)
                copy_y(UNITS - 1)

            def combine(f, b):
                step(v.scalar_tensor_tensor(x[:, b].rearrange("p t d -> p (t d)"), yall[:, b, 0:TILES, :].rearrange("p t d -> p (t d)"),
                                            0.5, x[:, b].rearrange("p t d -> p (t d)"), ALU.mult, ALU.add))
                v.wait_ge(gathered[b], 16 * 2 * TILES * (f + 1))
                for k in range(2):
                    for t in range(TILES):
                        last = v.scalar_tensor_tensor(x[:, b, t, :], got[:, b, k, t, :], gate[:, b, k, t:t + 1], x[:, b, t, :],
                                                      ALU.mult, ALU.add)
                    if k == 0:
                        step(last)
                return last

            def attn(b):
                n = ln_no[("attn", 0, b)]
                step(combine(0, b))
                norm(n, b)
                if b == 0:
                    v.wait_ge(qkv_in, 16 * 5)
                    v.tensor_scalar(bkg[:, :], const("gmask"), bias[:, 1:2], None, ALU.mult).then_inc(bkg_ready, 1)
                else:
                    v.wait_ge(v_stored, 16 * 5)
                for h in range(2):
                    v.wait_ge(v_proj, 2 * b + h + 1)
                    for g in range(HG):
                        last = v.tensor_tensor(vsb[:, 4 * h:4 * h + 4, g, 0:W],
                                               ps[:, misc[h], :].rearrange("p (t g n) -> p t g n", g=HG, n=W)[:, :, g, :],
                                               bv[:, g * W:(g + 1) * W].unsqueeze(1).to_broadcast([P, 4, W]), ALU.add)
                    last.then_inc(v_ready, 1)
                blk0, v0 = b * TILES, b * TILES * HG
                qmask = const("qmask").unsqueeze(1).to_broadcast([P, P, HG])

                def spread_q(blk, ring):
                    v.wait_ge(q_proj, blk + (blk0 + 1))
                    if not isinstance(blk, int) or blk0 + blk >= 2:
                        v.wait_ge(s_ready, (blk + (blk0 - 1)) * HG)
                    v.scalar_tensor_tensor(qbd[:, ring, :].rearrange("p (q h) -> p q h", h=HG),
                                           ps[:, 6, 0:P].unsqueeze(2).to_broadcast([P, P, HG]), bias[:, 0:1],
                                           qmask, ALU.add, ALU.mult).then_inc(q_ready, 1)

                def centre(i, k):
                    sc = ps[:, k, 0:CPB * KEYS].rearrange("p (c n) -> p c n", n=KEYS)
                    v.wait_ge(s_ready, i + (v0 + 1))
                    v.tensor_reduce(mx[:, k, :], sc, AX.X, ALU.max).then_inc(mx_ready, 1)
                    v.wait_ge(mx_ready, i + (v0 + 1))
                    if not isinstance(i, int) or v0 + i >= 2:
                        v.wait_ge(prob_ready, i + (v0 - 1))
                    v.tensor_tensor(cen[:, k], sc, mx[:, k, :].unsqueeze(2).to_broadcast([P, CPB, KEYS]), ALU.subtract)\
                     .then_inc(cen_ready, 1)

                def weigh(blk):
                    v.wait_ge(o_ready, (blk + blk0) * HG + HG)
                    half = HG // 2 * CPB
                    for z in range(2):
                        o = ps[:, 4 + z, 0:half * VG].rearrange("p (a n) -> p a n", n=VG)
                        last = v.reciprocal(rsum[:, z * half:(z + 1) * half], o[:, :, W])
                    last.then_inc(rsum_ready, 1)
                    v.wait_ge(rsum_ready, blk + (blk0 + 1))
                    v.tensor_tensor(rmask[:, :, :], rsum[:, :].unsqueeze(2).to_broadcast([P, HG * CPB, HG]),
                                    const("dmask").unsqueeze(1).to_broadcast([P, HG * CPB, HG]), ALU.mult).then_inc(rmask_ready, 1)
                    v.wait_ge(rmask_ready, blk + (blk0 + 1))
                    if not isinstance(blk, int) or blk0 + blk >= 1:
                        v.wait_ge(sel_ready, blk + blk0)
                    for z in range(2):
                        o = ps[:, 4 + z, 0:half * VG].rearrange("p (a n) -> p a n", n=VG)[:, :, 0:W]
                        v.tensor_tensor(omix[:, z * half:(z + 1) * half, :].rearrange("p a (h d) -> p a h d", d=HD),
                                        o.rearrange("p a (h d) -> p a h d", d=HD),
                                        rmask[:, z * half:(z + 1) * half, :].unsqueeze(3).to_broadcast([P, half, HG, HD]),
                                        ALU.mult).then_inc(omix_ready, 1)

                def residual(blk):
                    v.wait_ge(sel_ready, blk + (blk0 + 1))
                    xb = x[:, b, bass.ds(blk, 1), :].rearrange("p a n -> p (a n)")
                    v.tensor_tensor(xb, ps[:, 7, 0:D], xb, ALU.add).then_inc(x2_ready, 1)

                def unit(blk, g, ring):
                    later = not isinstance(blk, int) or blk >= 1
                    centre(blk * HG + g, g % 2)
                    if g == 1 and (not isinstance(blk, int) or blk + 1 < TILES):
                        spread_q(blk + 1, 1 - ring)
                    if g == 2 and later:
                        weigh(blk - 1)
                    if g == 3 and later:
                        residual(blk - 1)

                spread_q(0, 0)
                for g in range(HG):
                    unit(0, g, 0)
                with v.Fori(1, TILES - 2, 2) as blk:
                    for j in range(2):
                        for g in range(HG):
                            unit(blk + j, g, (1 + j) % 2)
                for g in range(HG):
                    unit(TILES - 1, g, (TILES - 1) % 2)
                weigh(TILES - 1)
                residual(TILES - 1)
                v.wait_ge(x2_ready, blk0 + TILES)

            for kind, f, b in STAGES:
                if kind == "route":
                    route(f, b)
                elif kind == "units":
                    units(f, b)
                elif kind == "attn":
                    attn(b)
                else:
                    combine(f, b).then_inc(x_done, 1)


def kernel(**inputs):
    import concourse.bacc as bacc
    from concourse.bass_utils import run_bass_kernel_spmd

    a = {k[3:]: np.asarray(v) for k, v in inputs.items()}
    up = np.concatenate([a["ffn_experts_w1"], a["ffn_shared_w1"][None]])
    down = np.concatenate([a["ffn_experts_w2"], a["ffn_shared_w2"][None]])
    arrays = {
        "x_in": a["attn_hidden_states"],
        "consts": shape_constants(),
        "w1t": up.transpose(2, 0, 1),
        "w2t": down.reshape(NEXP + 1, D, KCH, P).transpose(3, 0, 2, 1),
        "gate_wt": a["ffn_gate_w"].T,
        "wqt": a["attn_Wq"].T,
        "wkt": a["attn_Wk"].T,
        "wvt": a["attn_Wv"].T,
        "bqk": np.stack([a["attn_bq"], a["attn_bk"]], axis=1),
        "bv_rows": np.broadcast_to(a["attn_bv"], (P, D)),
    }
    arrays = {k: np.ascontiguousarray(v) for k, v in arrays.items()}
    nc = bacc.Bacc("TRN2", target_bir_lowering=False, num_devices=1)
    args = [nc.dram_tensor(k, v.shape, mybir.dt.from_np(v.dtype), kind="ExternalInput").ap() for k, v in arrays.items()]
    out = nc.dram_tensor("out", (B, S, D), mybir.dt.float32, kind="ExternalOutput").ap()
    macaron_kernel(nc, *args, out)
    r = run_bass_kernel_spmd(nc, [arrays], core_ids=[0])
    return r.results[0]["out"]
```

```python
import numpy as np
import concourse.bass as bass
from concourse import mybir
from contextlib import ExitStack

P = 128
B, S, D = 2, 1024, 128
HID, NEXP = 512, 8
SHARED = NEXP
TILES = S // P
KCH = HID // P
SLOT_TILES = (2 * S + NEXP * (P - 1)) // P
ROUTED = B * SLOT_TILES
UNITS = B * TILES + ROUTED
ROUTED0 = [B * TILES, 0]
SHARED0 = [0, ROUTED]
SHARED_BEFORE = [B * TILES, B * TILES]
HEADS, HD, W = 16, 8, 32
CHUNKS = S // W
CPB = P // W
HG = 4
KEYS = 3 * W
VG = W + 1
EPS = 1e-5
MASKED = -1.0e30

_WIDTHS = [("ident", P), ("tri", P), ("ones", P), ("sel", W), ("rep", P), ("beg", KEYS), ("end", KEYS),
           ("qmask", HG), ("gmask", HG), ("dmask", HG), ("rank", NEXP), ("cum", NEXP * NEXP), ("tile_no", SLOT_TILES),
           ("neg_half", TILES)]
CONST = {}
_at = 0
for _name, _w in _WIDTHS:
    CONST[_name] = (_at, _at + _w)
    _at += _w
NCONST = _at


def shape_constants():
    c = np.zeros((P, NCONST), np.float32)
    p = np.arange(P)

    def put(name, a):
        lo, hi = CONST[name]
        c[:, lo:hi] = np.asarray(a, np.float32).reshape(-1, hi - lo)

    put("ident", np.eye(P))
    put("tri", p[:, None] < p[None, :])
    put("ones", np.ones((P, P)))
    put("sel", (p[:, None] // HG) == np.arange(W)[None, :])
    put("rep", p[:, None] == (p[None, :] // HG))
    row, key = p[:, None] % W, np.arange(KEYS)[None, :]
    put("beg", np.where((key <= W) & (key < W - row), MASKED, 0.0))
    put("end", np.where((key >= 2 * W - 1) & (key - (2 * W - 1) >= W - row), MASKED, 0.0))
    inner = (p[:, None] % W) // HD == np.arange(HG)[None, :]
    put("qmask", inner * np.float32(1.0 / np.sqrt(HD)))
    put("gmask", p[:, None] // W == np.arange(HG)[None, :])
    put("dmask", p[:, None] % HG == np.arange(HG)[None, :])
    put("rank", np.tile(NEXP - np.arange(NEXP), (P, 1)))
    put("cum", np.tile((np.arange(NEXP)[None, :] <= np.arange(NEXP)[:, None]).ravel(), (P, 1)))
    put("tile_no", np.tile(np.arange(SLOT_TILES), (P, 1)))
    put("neg_half", np.full((P, TILES), -0.5))
    return c


def macaron_kernel(nc, x_in, consts, w1t, w2t, gate_wt, wqt, wkt, wvt, bqk, bv_rows, out):
    f32, bf16, i32 = mybir.dt.float32, mybir.dt.bfloat16, mybir.dt.int32
    ALU, ACT, AX = mybir.AluOpType, mybir.ActivationFunctionType, mybir.AxisListType

    ctx = ExitStack()
    with ctx:
        def sb(name, shape, dt=f32):
            return ctx.enter_context(nc.sbuf_tensor(name, shape, dt))

        def sem(name):
            return ctx.enter_context(nc.semaphore(name))

        rows = [nc.dram_tensor(f"expert_rows{b}", (SLOT_TILES * P, D), f32).ap() for b in range(B)]
        yrows = [nc.dram_tensor(f"expert_out{b}", (SLOT_TILES * P, D), f32).ap() for b in range(B)]
        vpad = [nc.dram_tensor(f"v_padded{b}", (S + 2 * W, HG * VG), f32).ap() for b in range(B)]

        cst = sb("cst", [P, NCONST])

        def const(name):
            lo, hi = CONST[name]
            return cst[:, lo:hi]

        ident, sel, rep = (const(n) for n in ("ident", "sel", "rep"))
        tri_bf, ones_bf = sb("tri_bf", [P, P], bf16), sb("ones_bf", [P, P], bf16)
        x = sb("x", [P, B * TILES, D])
        xn = sb("xn", [P, B * TILES, D])
        xnt = sb("xnt", [P, B * TILES, P])
        w1 = sb("w1", [P, NEXP + 1, HID])
        w2 = sb("w2", [P, NEXP + 1, KCH, D])
        gw = sb("gw", [P, NEXP])
        wq, wk, wv = sb("wq", [P, D]), sb("wk", [P, D]), sb("wv", [P, D])
        bias = sb("bias", [P, 2])
        bv = sb("bv", [P, D])
        zero = sb("zero", [P, D])

        stats = sb("stats", [P, TILES, 6])
        mv = sb("mv", [P, TILES, 2])
        vare = sb("vare", [P, TILES])
        rstd = sb("rstd", [P, TILES])

        logit = sb("logit", [P, TILES, NEXP])
        top = sb("top", [P, 2, TILES])
        hit = sb("hit", [P, TILES, NEXP])
        best = sb("best", [P, TILES])
        onehot = sb("onehot", [P, 2, TILES, NEXP])
        chosen = sb("chosen", [P, TILES + 1, NEXP], bf16)
        gap, egap = sb("gap", [P, TILES]), sb("egap", [P, TILES])
        rden = sb("rden", [P, TILES])
        gate = sb("gate", [P, B, 2, TILES])
        count = sb("count", [P, NEXP], i32)
        ntile = sb("ntile", [P, NEXP])
        ends8 = sb("ends8", [P, NEXP, NEXP])
        end_tile = sb("end_tile", [P, NEXP])
        base = sb("base", [P, NEXP])
        slot = sb("slot", [P, TILES, NEXP])
        slot2 = sb("slot2", [P, 2, TILES, NEXP])
        slotf = sb("slotf", [P, 2, TILES])
        slot_i = sb("slot_i", [P, B, 2, TILES], i32)
        passed = sb("passed", [1, SLOT_TILES, NEXP])
        tile_ef = sb("tile_ef", [1, SLOT_TILES])
        tile_e = sb("tile_e", [1, ROUTED], i32)

        xrow = sb("xrow", [P, 4, D])
        xt = sb("xt", [P, 2, P])
        th = sb("th", [P, 2, HID])
        act = sb("act", [P, 2, HID])
        act_t = sb("act_t", [P, 2, KCH * P])
        yall = sb("yall", [P, ROUTED, D])
        got = sb("got", [P, 2, TILES, D])

        kt = sb("kt", [P, B, HG, S + 2 * W])
        bkg = sb("bkg", [P, HG])
        vsb = sb("vsb", [P, TILES, HG, VG])
        vend = sb("vend", [W, HG, VG])
        vwin = sb("vwin", [KEYS, B, CHUNKS, HG * VG])
        qbd = sb("qbd", [P, 2, P * HG])
        mx = sb("mx", [P, 2, CPB])
        cen = sb("cen", [P, 2, CPB, KEYS])
        prob = sb("prob", [P, 2, CPB, KEYS])
        prob_t = sb("prob_t", [KEYS, 2, CPB * P])
        HALF = HG // 2 * CPB
        rsum = sb("rsum", [P, 2, HALF])
        rmask = sb("rmask", [P, 2, HALF, HG])
        omix = sb("omix", [P, 2, HALF, W])

        ps = ctx.enter_context(nc.psum_tensor("ps", [P, 8, 512], f32))
        H_BANK = S_BANK = 0
        TURN_BANK, ROW_BANK, Y_BANK, O_BANK = 2, 3, 4, 4
        Q_BANK = PICK_BANK = 6
        PICK_AT = P
        SIDE_RUN, SIDE_ATTN = (6, 7), (3, 7)

        const_in, w_shared_in, w_in, qkv_in, zeroed = (sem(n) for n in ("const_in", "w_shared_in", "w_in", "qkv_in", "zeroed"))
        x_arrived = [sem(f"x_arrived{b}") for b in range(B)]
        zero_set, preset, bf_ready = sem("zero_set"), sem("preset"), sem("bf_ready")
        dve_step = sem("dve_step")
        vare_ready, rstd_ready, xn_ready = sem("vare_ready"), sem("rstd_ready"), sem("xn_ready")
        half_turned, half_copied = sem("half_turned"), sem("half_copied")
        logits_ready, chosen_ready, pos_ready = sem("logits_ready"), sem("chosen_ready"), sem("pos_ready")
        gap_ready, egap_ready, route_ready = sem("gap_ready"), sem("egap_ready"), sem("route_ready")
        scattered = [sem(f"scattered{b}") for b in range(B)]
        row_in = [sem(f"row_in{i}") for i in range(4)]
        xt_turned, xt_ready, h_ready, th_ready, act_ready = (sem(n) for n in ("xt_turned", "xt_ready", "h_ready", "th_ready", "act_ready"))
        act_turned, act_t_ready, y_ready, y_copied = (sem(n) for n in ("act_turned", "act_t_ready", "y_ready", "y_copied"))
        y_stored = [sem(f"y_stored{b}") for b in range(B)]
        gathered = [sem(f"gathered{t}") for t in range(TILES)]
        k_proj, k_ready, v_proj, v_ready, v_stored, vwin_in = (sem(n) for n in ("k_proj", "k_ready", "v_proj", "v_ready", "v_stored", "vwin_in"))
        q_proj, q_ready, s_ready, mx_ready, cen_ready, prob_ready = (sem(n) for n in ("q_proj", "q_ready", "s_ready", "mx_ready", "cen_ready", "prob_ready"))
        prob_turned, prob_t_ready, o_ready, omix_ready, sel_ready, x2_ready = (sem(n) for n in ("prob_turned", "prob_t_ready", "o_ready", "omix_ready", "sel_ready", "x2_ready"))
        rsum_ready, rmask_ready, bkg_ready = sem("rsum_ready"), sem("rmask_ready"), sem("bkg_ready")
        combined, stored = sem("combined"), sem("stored")

        GROUPS = [(lo, min(lo + 4, SLOT_TILES)) for lo in range(0, SLOT_TILES, 4)]
        V_PAD = 2 * B
        AU = TILES * HG

        R0B0, R0B1, A_B0, A_B1, R1B0, R1B1 = range(6)

        def routed(r, i):
            return ROUTED0[r] <= i < ROUTED0[r] + ROUTED

        def unit_no(r, i):
            return r * UNITS + i

        def routed_no(r, i):
            return r * ROUTED + (i - ROUTED0[r])

        block = ctx.enter_context(nc.Block())

        @block.sync
        def _(sp):
            sp.dma_start(x[:, 0:TILES], x_in[0].rearrange("(t p) d -> p t d", p=P)).then_inc(x_arrived[0], 16)
            sp.dma_start(w1[:, SHARED], w1t[:, SHARED]).then_inc(w_shared_in, 16)
            sp.dma_start(w2[:, SHARED], w2t[:, SHARED]).then_inc(w_shared_in, 16)
            sp.dma_start(x[:, TILES:], x_in[1].rearrange("(t p) d -> p t d", p=P)).then_inc(x_arrived[1], 16)
            sp.dma_start(w1[:, 0:NEXP], w1t[:, 0:NEXP]).then_inc(w_in, 16)
            sp.dma_start(w2[:, 0:NEXP], w2t[:, 0:NEXP]).then_inc(w_in, 16)
            for dst, src in ((wq, wqt), (wk, wkt), (wv, wvt), (bias, bqk), (bv, bv_rows)):
                sp.dma_start(dst[:, :], src).then_inc(qkv_in, 16)
            sp.wait_ge(preset, 3)
            for b in range(B):
                for at in (0, S + W):
                    sp.dma_start(vpad[b][at:at + W, :], vend[:, :, :].rearrange("p g n -> p (g n)")).then_inc(v_stored, 16)

            def load_rows(r, b, lo, n):
                for j in range(n):
                    no = r * ROUTED + b * SLOT_TILES + lo + j
                    if not isinstance(lo, int) or no >= 4:
                        sp.wait_ge(xt_turned, no - 3)
                    k = no % 4 if isinstance(lo, int) else (r * ROUTED + b * SLOT_TILES + j) % 4
                    sp.dma_start(xrow[:, k], rows[b][bass.ds((lo + j) * P, P), :]).then_inc(row_in[k], 16)

            def store_y(r, b, lo, n):
                sp.wait_ge(y_copied, lo + (unit_no(r, ROUTED0[r]) + b * SLOT_TILES + n))
                sp.dma_start(yrows[b][bass.ds(lo * P, n * P), :].rearrange("(t p) d -> p t d", p=P),
                             yall[:, bass.ds(lo + b * SLOT_TILES, n), :]).then_inc(y_stored[b], 16)

            def last_stores(r, b, groups):
                for lo, hi in groups:
                    store_y(r, b, lo, hi - lo)

            def routed_tiles(r, b):
                sp.wait_ge(scattered[b], 16 * 2 * TILES * (r + 1))
                load_rows(r, b, 0, 4)
                if b:
                    last_stores(r, 0, GROUPS[3:4])
                load_rows(r, b, 4, 4)
                if b:
                    last_stores(r, 0, GROUPS[4:])
                with sp.Fori(8, SLOT_TILES - 3 - 3, 4) as lo:
                    load_rows(r, b, lo, 4)
                    store_y(r, b, lo - 8, 4)
                load_rows(r, b, SLOT_TILES - 3, 3)

            def values(b):
                sp.wait_ge(v_ready, 2 * (b + 1))
                sp.dma_start(vpad[b][W:W + S, :].rearrange("(t p) n -> p t n", p=P),
                             vsb[:, :, :, :].rearrange("p t g n -> p t (g n)")).then_inc(v_stored, 16)
                sp.wait_ge(v_stored, 16 * (V_PAD + b + 1))
                for part in range(3):
                    sp.dma_start(vwin[part * W:(part + 1) * W, b, :, :],
                                 vpad[b][part * W:part * W + S, :].rearrange("(c p) n -> p c n", p=W)).then_inc(vwin_in, 16)

            assert len(GROUPS) == 6
            routed_tiles(0, 0)
            routed_tiles(0, 1)
            last_stores(0, 1, GROUPS[3:4])
            values(0)
            last_stores(0, 1, GROUPS[4:])
            values(1)
            routed_tiles(1, 0)
            routed_tiles(1, 1)
            last_stores(1, 1, GROUPS[3:])
            for b in range(B):
                for h in range(2):
                    lo, n = h * TILES // 2, TILES // 2
                    sp.wait_ge(y_copied, unit_no(1, SHARED0[1]) + b * TILES + lo + n)
                    sp.dma_start(out[b, lo * P:(lo + n) * P].rearrange("(t p) d -> p t d", p=P),
                                 x[:, b * TILES + lo:b * TILES + lo + n]).then_inc(stored, 16)
            sp.wait_ge(stored, 16 * 2 * B)

        @block.gpsimd
        def _(pool):
            pool.memset(zero[:, :], 0.0).then_inc(zero_set, 1)
            pool.memset(chosen[:, TILES, :], 0.0).then_inc(preset, 1)
            pool.memset(vend[:, :, 0:W], 0.0).then_inc(preset, 1)
            pool.memset(vend[:, :, W:VG], 1.0).then_inc(preset, 1)

            def norm(n):
                pool.wait_ge(vare_ready, n + 1)
                if n == 0:
                    pool.wait_ge(const_in, 32)
                pool.tensor_tensor(rstd[:, :], vare[:, :], const("neg_half"), ALU.pow).then_inc(rstd_ready, 1)

            def scatter(f, b):
                pool.wait_ge(route_ready, f * B + b + 1)
                if f == 0:
                    pool.wait_ge(zeroed, 16 * B)
                for t in range(TILES):
                    for k in range(2):
                        pool.indirect_dma_start(
                            out=rows[b], out_offset=bass.IndirectOffsetOnAxis(ap=slot_i[:, b, k, t:t + 1], axis=0),
                            in_=xn[:, b * TILES + t, :], in_offset=None).then_inc(scattered[b], 16)

            def gather(f, b):
                if f * B + b:
                    pool.wait_ge(combined, (f * B + b) * TILES)
                pool.wait_ge(y_stored[b], 16 * len(GROUPS) * (f + 1))
                for t in range(TILES):
                    for k in range(2):
                        pool.indirect_dma_start(
                            out=got[:, k, t, :], out_offset=None, in_=yrows[b],
                            in_offset=bass.IndirectOffsetOnAxis(ap=slot_i[:, b, k, t:t + 1], axis=0)).then_inc(gathered[t], 16)

            norm(R0B0)
            pool.memset(vsb[:, :, :, W:VG], 1.0).then_inc(preset, 1)
            pool.memset(kt[:, :, :, 0:W], 0.0).then_inc(preset, 1)
            pool.memset(kt[:, :, :, W + S:], 0.0).then_inc(preset, 1)
            scatter(0, 0)
            norm(R0B1)
            scatter(0, 1)
            gather(0, 0)
            norm(A_B0)
            gather(0, 1)
            norm(A_B1)
            norm(R1B0)
            scatter(1, 0)
            norm(R1B1)
            scatter(1, 1)
            gather(1, 0)
            gather(1, 1)

        @block.scalar
        def _(s):
            s.dma_start(cst[:, :], consts).then_inc(const_in, 16)
            s.dma_start(gw[:, :], gate_wt).then_inc(const_in, 16)
            s.wait_ge(zero_set, 1)
            s.wait_ge(x_arrived[1], 16)
            for b in range(B):
                s.dma_start(rows[b].rearrange("(t p) d -> p t d", p=P),
                            zero[:, :].unsqueeze(1).to_broadcast([P, SLOT_TILES, D])).then_inc(zeroed, 16)

            def copy_halves(n, b, banks):
                for h in range(2):
                    s.wait_ge(half_turned, 2 * n + h + 1)
                    lo = b * TILES + 4 * h
                    s.activation(xnt[:, lo:lo + 4, :].rearrange("p t n -> p (t n)"), ps[:, banks[h], :], ACT.Copy).then_inc(half_copied, 1)

            def exp_gap(r):
                s.wait_ge(gap_ready, r + 1)
                s.activation(egap[:, :], gap[:, :], ACT.Exp).then_inc(egap_ready, 1)

            def keys(b, banks):
                if b == 0:
                    s.wait_ge(preset, 6)
                    s.wait_ge(bkg_ready, 1)
                for h in range(2):
                    s.wait_ge(k_proj, 2 * b + h + 1)
                    for g in range(HG):
                        last = s.activation(kt[:, b, g, W + h * 512:W + (h + 1) * 512], ps[:, banks[h], :], ACT.Identity,
                                            bias=bkg[:, g:g + 1], scale=const("gmask")[:, g:g + 1])
                    last.then_inc(k_ready, 1)

            def copy_act(no, k):
                s.wait_ge(act_turned, no + 1)
                if not isinstance(no, int) or no >= 2:
                    s.wait_ge(y_ready, no - 1)
                s.activation(act_t[:, k, :], ps[:, TURN_BANK, :], ACT.Copy, scale=0.5).then_inc(act_t_ready, 1)

            def tanh(no, k):
                s.wait_ge(h_ready, no + 1)
                if not isinstance(no, int) or no >= 2:
                    s.wait_ge(act_ready, no - 1)
                s.activation(th[:, k, :], ps[:, H_BANK + k, :], ACT.Tanh, scale=0.5).then_inc(th_ready, 1)

            def units(r, lo, hi):
                def unit(i, k):
                    if not (isinstance(i, int) and i < 2):
                        copy_act(i + (unit_no(r, 0) - 2), k)
                    tanh(i + unit_no(r, 0), k)
                while r == 0 and lo < min(4, hi):
                    unit(lo, lo % 2)
                    lo += 1
                if hi - lo >= 6:
                    even = lo + (hi - lo) // 2 * 2
                    with s.Fori(lo, even - 1, 2) as i:
                        for j in range(2):
                            unit(i + j, (lo + j) % 2)
                    lo = even
                for i in range(lo, hi):
                    unit(i, i % 2)

            def drain(r):
                for i in range(UNITS - 2, UNITS):
                    copy_act(unit_no(r, i), i % 2)

            def exp(no, k):
                s.wait_ge(cen_ready, no + 1)
                if not isinstance(no, int) or no >= 2:
                    s.wait_ge(prob_turned, no - 1)
                s.activation(prob[:, k], cen[:, k], ACT.Exp).then_inc(prob_ready, 1)

            def copy_prob(no, k):
                s.wait_ge(prob_turned, no + 1)
                if not isinstance(no, int) or no >= 2:
                    s.wait_ge(o_ready, no - 1)
                s.activation(prob_t[:, k, :], ps[0:KEYS, TURN_BANK, :], ACT.Copy).then_inc(prob_t_ready, 1)

            def attn(b, lo, hi):
                v0 = b * AU

                def unit(v, k):
                    exp(v + v0, k)
                    if not (isinstance(v, int) and v == 0):
                        copy_prob(v + (v0 - 1), 1 - k)
                while b == 0 and lo < min(4, hi):
                    unit(lo, lo % 2)
                    lo += 1
                if hi - lo >= 6 and lo >= 1:
                    even = lo + (hi - lo) // 2 * 2
                    with s.Fori(lo, even - 1, 2) as v:
                        for j in range(2):
                            unit(v + j, (lo + j) % 2)
                    lo = even
                for v in range(lo, hi):
                    unit(v, v % 2)

            copy_halves(R0B0, 0, SIDE_RUN)
            units(0, 0, 2)
            exp_gap(0)
            units(0, 2, 8)
            copy_halves(R0B1, 1, SIDE_RUN)
            units(0, 8, 10)
            exp_gap(1)
            units(0, 10, 58)
            copy_halves(A_B0, 0, SIDE_RUN)
            units(0, 58, 59)
            keys(0, SIDE_RUN)
            units(0, 59, UNITS)
            drain(0)
            attn(0, 0, 26)
            copy_halves(A_B1, 1, SIDE_ATTN)
            attn(0, 26, 27)
            keys(1, SIDE_ATTN)
            attn(0, 27, AU)
            copy_prob(AU - 1, 1)
            attn(1, 0, 5)
            copy_halves(R1B0, 0, SIDE_ATTN)
            attn(1, 5, 9)
            exp_gap(2)
            attn(1, 9, AU)
            copy_prob(2 * AU - 1, 1)
            units(1, 0, 4)
            copy_halves(R1B1, 1, SIDE_RUN)
            units(1, 4, 6)
            exp_gap(3)
            units(1, 6, UNITS)
            drain(1)

        @block.tensor
        def _(pe):
            def turn_halves(n, b, banks):
                pe.wait_ge(xn_ready, n + 1)
                for h in range(2):
                    for t in range(4):
                        last = pe.transpose(ps[:, banks[h], t * P:(t + 1) * P], xn[:, b * TILES + 4 * h + t, :], ident)
                    last.then_inc(half_turned, 1)

            def logits(n, b, banks):
                pe.wait_ge(half_copied, 2 * n + 2)
                for t in range(TILES):
                    last = pe.matmul(ps[:, banks[0], t * NEXP:(t + 1) * NEXP], xnt[:, b * TILES + t, :], gw[:, :],
                                     start=True, stop=True)
                last.then_inc(logits_ready, 1)

            def ranks(r, banks):
                pe.wait_ge(chosen_ready, r + 1)
                for t in range(TILES):
                    pe.matmul(ps[:, banks[1], (t + 1) * NEXP:(TILES + 1) * NEXP].rearrange("p (t e) -> p t e", e=NEXP),
                              ones_bf[:, :], chosen[:, t:t + 1, :].to_broadcast([P, TILES - t, NEXP]),
                              start=(t == 0), stop=False, skip_group_check=True)
                pe.matmul(ps[:, banks[1], 0:(TILES + 1) * NEXP], tri_bf[:, :], chosen[:, :, :].rearrange("p t e -> p (t e)"),
                          start=False, stop=True, skip_group_check=True).then_inc(pos_ready, 1)

            def key_proj(n, b, banks):
                pe.wait_ge(half_copied, 2 * n + 2)
                if b == 0:
                    pe.wait_ge(qkv_in, 16 * 5)
                for h in range(2):
                    lo = b * TILES + 4 * h
                    pe.matmul(ps[:, banks[h], :], wk[:, :], xnt[:, lo:lo + 4, :].rearrange("p t n -> p (t n)"),
                              start=True, stop=True).then_inc(k_proj, 1)

            def value_proj(b, banks):
                for h in range(2):
                    pe.wait_ge(k_ready, 2 * b + h + 1)
                    for t in range(4):
                        last = pe.matmul(ps[:, banks[h], t * P:(t + 1) * P], xnt[:, b * TILES + 4 * h + t, :], wv[:, :],
                                         start=True, stop=True)
                    last.then_inc(v_proj, 1)

            expert = {}

            def turn_rows(r, i):
                no = routed_no(r, i)
                pe.wait_ge(row_in[no % 4], 16 * (no // 4 + 1))
                if no >= 1:
                    pe.wait_ge(xt_ready, no)
                pe.transpose(ps[:, ROW_BANK, 0:P], xrow[:, no % 4, :], ident).then_inc(xt_turned, 1)
                x_at = i - ROUTED0[r]
                expert[i] = pe.value_load(tile_e[0:1, x_at:x_at + 1], min_val=0, max_val=NEXP - 1)

            def up(r, i):
                no = unit_no(r, i)
                if no >= 2:
                    pe.wait_ge(act_ready, no - 1)
                if routed(r, i):
                    pe.wait_ge(xt_ready, routed_no(r, i) + 1)
                    pe.matmul(ps[:, H_BANK + i % 2, :], xt[:, routed_no(r, i) % 2, :],
                              w1[:, bass.ds(expert[i], 1), :].rearrange("p a n -> p (a n)"), start=True, stop=True)\
                      .then_inc(h_ready, 1)
                else:
                    pe.matmul(ps[:, H_BANK + i % 2, :], xnt[:, i - SHARED0[r], :], w1[:, SHARED, :], start=True, stop=True)\
                      .then_inc(h_ready, 1)

            def down(r, i):
                no = unit_no(r, i)
                pe.wait_ge(act_t_ready, no + 1)
                if no >= 2:
                    pe.wait_ge(y_copied, no - 1)
                for c in range(KCH):
                    w = w2[:, bass.ds(expert[i], 1), c, :].rearrange("p a n -> p (a n)") if routed(r, i) else w2[:, SHARED, c, :]
                    last = pe.matmul(ps[:, Y_BANK + i % 2, 0:D], act_t[:, i % 2, c * P:(c + 1) * P], w,
                                     start=(c == 0), stop=(c == KCH - 1))
                last.then_inc(y_ready, 1)
                expert.pop(i, None)

            def turn_act(r, i):
                no = unit_no(r, i)
                pe.wait_ge(act_ready, no + 1)
                if no >= 1:
                    pe.wait_ge(act_t_ready, no)
                for c in range(KCH):
                    last = pe.transpose(ps[:, TURN_BANK, c * P:(c + 1) * P], act[:, i % 2, c * P:(c + 1) * P], ident)
                last.then_inc(act_turned, 1)

            def units(r, lo, hi):
                for i in range(lo, hi):
                    if i < UNITS:
                        up(r, i)
                    if i + 1 < UNITS and routed(r, i + 1):
                        turn_rows(r, i + 1)
                    if i >= 2:
                        down(r, i - 2)
                    if 1 <= i <= UNITS:
                        turn_act(r, i - 1)

            def q_block(b, blk):
                no = b * TILES + blk
                if no:
                    pe.wait_ge(q_ready, no)
                if max(no - 2, b * TILES) > 0:
                    pe.wait_ge(x2_ready, max(no - 2, b * TILES))
                pe.matmul(ps[:, Q_BANK, 0:P], wq[:, :], xnt[:, b * TILES + blk, :], start=True, stop=True).then_inc(q_proj, 1)

            def scores(b, v):
                blk, g, no = v // HG, v % HG, b * AU + v
                if g == 0:
                    pe.wait_ge(q_ready, b * TILES + blk + 1)
                if no >= 2:
                    pe.wait_ge(cen_ready, no - 1)
                for c in range(CPB):
                    mask = "beg" if v < HG and c == 0 else "end" if v >= AU - HG and c == CPB - 1 else None
                    dst = ps[:, S_BANK + v % 2, c * KEYS:(c + 1) * KEYS]
                    at = blk * P + c * W
                    last = pe.matmul(dst, qbd[:, blk % 2, c * P:(c + 1) * P], kt[:, b, g, at:at + KEYS],
                                     start=True, stop=(mask is None))
                    if mask:
                        last = pe.matmul(dst, rep, const(mask), start=False, stop=True)
                last.then_inc(s_ready, 1)

            def turn_prob(b, v):
                no = b * AU + v
                pe.wait_ge(prob_ready, no + 1)
                if no >= 1:
                    pe.wait_ge(prob_t_ready, no)
                for c in range(CPB):
                    last = pe.transpose(ps[0:KEYS, TURN_BANK, c * P:(c + 1) * P], prob[:, v % 2, c, :], ident)
                last.then_inc(prob_turned, 1)

            def mix(b, v):
                blk, g, no = v // HG, v % HG, b * AU + v
                half = no // 2
                pe.wait_ge(prob_t_ready, no + 1)
                if g % 2 == 0 and half >= 2:
                    pe.wait_ge(omix_ready, half - 1)
                for c in range(CPB):
                    at = ((g % 2) * CPB + c) * VG
                    last = pe.matmul(ps[:, O_BANK + half % 2, at:at + VG], prob_t[:, v % 2, c * P:(c + 1) * P],
                                     vwin[:, b, blk * CPB + c, g * VG:(g + 1) * VG], start=True, stop=True)
                last.then_inc(o_ready, 1)

            def pick(b, blk):
                no = b * TILES + blk
                pe.wait_ge(omix_ready, 2 * no + 2)
                pe.wait_ge(q_ready, min(no + 3, (b + 1) * TILES))
                if no >= 1:
                    pe.wait_ge(x2_ready, no)
                for c in range(CPB):
                    last = pe.matmul(ps[c * W:(c + 1) * W, PICK_BANK, PICK_AT:PICK_AT + D], sel,
                                     omix[:, :, :, :].rearrange("p z (g c) n -> p (z g) c n", c=CPB)[:, :, c, :],
                                     start=True, stop=True)
                last.then_inc(sel_ready, 1)

            def attn(b, lo, hi):
                for v in range(lo, hi):
                    if v < AU:
                        scores(b, v)
                    if v % HG == 3 and v >= HG:
                        pick(b, v // HG - 1)
                    if v >= 2:
                        mix(b, v - 2)
                    if 1 <= v <= AU:
                        turn_prob(b, v - 1)
                    if v % HG == 1 and v // HG + 1 < TILES:
                        q_block(b, v // HG + 1)

            pe.wait_ge(const_in, 32)
            turn_halves(R0B0, 0, SIDE_RUN)
            logits(R0B0, 0, SIDE_RUN)
            pe.wait_ge(w_shared_in, 16 * 2)
            units(0, 0, 3)
            pe.wait_ge(bf_ready, 2)
            ranks(0, SIDE_RUN)
            units(0, 3, 7)
            turn_halves(R0B1, 1, SIDE_RUN)
            units(0, 7, 8)
            logits(R0B1, 1, SIDE_RUN)
            units(0, 8, 11)
            ranks(1, SIDE_RUN)
            units(0, 11, ROUTED0[0] - 1)
            pe.wait_ge(route_ready, B)
            pe.wait_ge(w_in, 16 * 2)
            units(0, ROUTED0[0] - 1, 57)
            turn_halves(A_B0, 0, SIDE_RUN)
            units(0, 57, 58)
            key_proj(A_B0, 0, SIDE_RUN)
            units(0, 58, 60)
            value_proj(0, SIDE_RUN)
            units(0, 60, UNITS + 2)
            pe.wait_ge(act_t_ready, UNITS)
            pe.wait_ge(y_copied, UNITS)
            pe.wait_ge(v_ready, 2)
            q_block(0, 0)
            attn(0, 0, 2)
            pe.wait_ge(vwin_in, 16 * 3)
            attn(0, 2, 26)
            turn_halves(A_B1, 1, SIDE_ATTN)
            attn(0, 26, 27)
            key_proj(A_B1, 1, SIDE_ATTN)
            attn(0, 27, 28)
            value_proj(1, SIDE_ATTN)
            attn(0, 28, AU + 2)
            pick(0, TILES - 1)
            q_block(1, 0)
            attn(1, 0, 2)
            pe.wait_ge(vwin_in, 16 * 3 * 2)
            attn(1, 2, 5)
            turn_halves(R1B0, 0, SIDE_ATTN)
            attn(1, 5, 6)
            logits(R1B0, 0, SIDE_ATTN)
            attn(1, 6, 10)
            ranks(2, SIDE_ATTN)
            attn(1, 10, AU + 2)
            pick(1, TILES - 1)
            pe.wait_ge(route_ready, 3)
            pe.wait_ge(x2_ready, B * TILES)
            turn_rows(1, 0)
            units(1, 0, 4)
            turn_halves(R1B1, 1, SIDE_RUN)
            logits(R1B1, 1, SIDE_RUN)
            units(1, 4, 7)
            ranks(3, SIDE_RUN)
            units(1, 7, SLOT_TILES - 1)
            pe.wait_ge(route_ready, 4)
            units(1, SLOT_TILES - 1, UNITS + 2)

        @block.vector
        def _(v):
            steps = [0]

            def step(ins):
                steps[0] += 1
                ins.then_inc(dve_step, 1)
                v.wait_ge(dve_step, steps[0])

            def norm_stats(b):
                for t in range(TILES):
                    last = v.bn_stats(stats[:, t, :], x[:, b * TILES + t, :])
                step(last)

            def norm_var(b):
                for t in range(TILES):
                    last = v.bn_aggr(mv[:, t, :], stats[:, t, :])
                step(last)
                v.tensor_scalar(vare[:, :], mv[:, :, 1], EPS, None, ALU.add).then_inc(vare_ready, 1)

            def norm_apply(n, b):
                v.wait_ge(rstd_ready, n + 1)
                for t in range(TILES):
                    last = v.tensor_scalar(xn[:, b * TILES + t, :], x[:, b * TILES + t, :], mv[:, t, 0:1], rstd[:, t:t + 1],
                                           ALU.subtract, ALU.mult)
                last.then_inc(xn_ready, 1)

            def over_experts(a):
                return a.unsqueeze(2).to_broadcast([P, TILES, NEXP])

            rank = const("rank").unsqueeze(1).to_broadcast([P, TILES, NEXP])

            def choose(k):
                step(v.tensor_reduce(top[:, k, :], logit[:, :, :], AX.X, ALU.max))
                step(v.tensor_tensor(hit[:, :, :], logit[:, :, :], over_experts(top[:, k, :]), ALU.is_equal))
                step(v.tensor_tensor(hit[:, :, :], hit[:, :, :], rank, ALU.mult))
                step(v.tensor_reduce(best[:, :], hit[:, :, :], AX.X, ALU.max))
                step(v.tensor_tensor(onehot[:, k], rank, over_experts(best[:, :]), ALU.is_equal))

            def first_choice(r, banks):
                v.wait_ge(logits_ready, r + 1)
                step(v.tensor_copy(logit[:, :, :], ps[:, banks[0], 0:TILES * NEXP].rearrange("p (t e) -> p t e", e=NEXP)))
                choose(0)

            def second_choice():
                step(v.scalar_tensor_tensor(logit[:, :, :], onehot[:, 0], -3.0e38, logit[:, :, :], ALU.mult, ALU.add))
                choose(1)
                v.tensor_tensor(chosen[:, 0:TILES, :], onehot[:, 0], onehot[:, 1], ALU.add).then_inc(chosen_ready, 1)
                v.tensor_tensor(gap[:, :], top[:, 1, :], top[:, 0, :], ALU.subtract).then_inc(gap_ready, 1)

            def gates(r, b):
                v.wait_ge(egap_ready, r + 1)
                step(v.tensor_scalar(rden[:, :], egap[:, :], 1.0, None, ALU.add))
                step(v.reciprocal(rden[:, :], rden[:, :]))
                step(v.tensor_scalar(gate[:, b, 0, :], rden[:, :], 0.5, None, ALU.mult))
                step(v.tensor_tensor(gate[:, b, 1, :], gate[:, b, 0, :], egap[:, :], ALU.mult))

            def expert_tiles(r, b, banks):
                v.wait_ge(pos_ready, r + 1)
                step(v.tensor_scalar(count[:, :], ps[:, banks[1], TILES * NEXP:(TILES + 1) * NEXP], float(P - 1), None, ALU.add))
                step(v.tensor_scalar(count[:, :], count[:, :], P.bit_length() - 1, None, ALU.logical_shift_right))
                step(v.tensor_copy(ntile[:, :], count[:, :]))
                step(v.tensor_tensor(ends8[:, :, :], ntile[:, :].unsqueeze(1).to_broadcast([P, NEXP, NEXP]),
                                     const("cum").rearrange("p (a c) -> p a c", c=NEXP), ALU.mult))
                step(v.tensor_reduce(end_tile[:, :], ends8[:, :, :], AX.X, ALU.add))
                step(v.tensor_tensor(passed[:, :, :], end_tile[0:1, :].unsqueeze(1).to_broadcast([1, SLOT_TILES, NEXP]),
                                     const("tile_no")[0:1, :].unsqueeze(2).to_broadcast([1, SLOT_TILES, NEXP]), ALU.is_le))
                step(v.tensor_reduce(tile_ef[:, :], passed[:, :, :], AX.X, ALU.add))
                step(v.tensor_scalar(tile_e[:, b * SLOT_TILES:(b + 1) * SLOT_TILES], tile_ef[:, :], float(NEXP - 1), None, ALU.min))

            def expert_rows(b, banks):
                pos = ps[:, banks[1], 0:TILES * NEXP].rearrange("p (t e) -> p t e", e=NEXP)
                step(v.tensor_tensor(base[:, :], end_tile[:, :], ntile[:, :], ALU.subtract))
                step(v.tensor_scalar(base[:, :], base[:, :], float(P), None, ALU.mult))
                step(v.tensor_tensor(slot[:, :, :], pos, base[:, :].unsqueeze(1).to_broadcast([P, TILES, NEXP]), ALU.add))
                for k in range(2):
                    step(v.tensor_tensor(slot2[:, k], slot[:, :, :], onehot[:, k], ALU.mult))
                step(v.tensor_reduce(slotf[:, :, :], slot2[:, :, :, :], AX.X, ALU.add))
                v.tensor_copy(slot_i[:, b, :, :], slotf[:, :, :]).then_inc(route_ready, 1)

            def combine(f, b, t):
                v.wait_ge(gathered[t], 16 * 2 * (f * B + b + 1))
                xs = x[:, b * TILES + t, :]
                step(v.scalar_tensor_tensor(xs, got[:, 0, t, :], gate[:, b, 0, t:t + 1], xs, ALU.mult, ALU.add))
                v.scalar_tensor_tensor(xs, got[:, 1, t, :], gate[:, b, 1, t:t + 1], xs, ALU.mult, ALU.add).then_inc(combined, 1)
                v.wait_ge(combined, (f * B + b) * TILES + t + 1)

            def copy_xt(r, no, k):
                v.wait_ge(xt_turned, no + 1)
                if not isinstance(no, int) or no >= 2:
                    v.wait_ge(h_ready, no - 1 + SHARED_BEFORE[r])
                v.tensor_copy(xt[:, k, :], ps[:, ROW_BANK, 0:P]).then_inc(xt_ready, 1)

            def silu(no, k):
                v.wait_ge(th_ready, no + 1)
                if not isinstance(no, int) or no >= 2:
                    v.wait_ge(act_turned, no - 1)
                v.scalar_tensor_tensor(act[:, k, :], th[:, k, :], 1.0, ps[:, H_BANK + k, :], ALU.add, ALU.mult).then_inc(act_ready, 1)

            def take_y(r, i, k, is_routed):
                v.wait_ge(y_ready, i + (unit_no(r, 0) + 1))
                y = ps[:, Y_BANK + k, 0:D]
                if is_routed:
                    at = i - ROUTED0[r]
                    v.tensor_copy(yall[:, bass.ds(at, 1), :].rearrange("p a n -> p (a n)"), y).then_inc(y_copied, 1)
                else:
                    xs = x[:, i - SHARED0[r], :]
                    if r == 1:
                        v.wait_ge(combined, (2 * B - 1) * TILES + max(0, i - SHARED0[1] - TILES + 1))
                    v.scalar_tensor_tensor(xs, y, 0.5, xs, ALU.mult, ALU.add).then_inc(y_copied, 1)

            def unit(r, i):
                if i + 1 < UNITS and routed(r, i + 1):
                    copy_xt(r, routed_no(r, i + 1), (i + 1) % 2)
                silu(unit_no(r, i), i % 2)
                if i >= 2:
                    take_y(r, i - 2, i % 2, routed(r, i - 2))

            def routed_units(r, lo, hi):
                assert (hi - lo) % 2 == 0 and routed(r, lo - 2) and routed(r, hi)
                with v.Fori(lo, hi - 1, 2) as i:
                    for j in range(2):
                        k = (lo + j) % 2
                        copy_xt(r, i + (routed_no(r, 0) + j + 1), 1 - k)
                        silu(i + (unit_no(r, 0) + j), k)
                        take_y(r, i + (j - 2), k, True)

            def drain(r):
                for i in range(UNITS - 2, UNITS):
                    take_y(r, i, i % 2, routed(r, i))

            qmask = const("qmask").unsqueeze(1).to_broadcast([P, P, HG])

            def values(b, banks):
                for h in range(2):
                    v.wait_ge(v_proj, 2 * b + h + 1)
                    for g in range(HG):
                        last = v.tensor_tensor(vsb[:, 4 * h:4 * h + 4, g, 0:W],
                                               ps[:, banks[h], :].rearrange("p (t g n) -> p t g n", g=HG, n=W)[:, :, g, :],
                                               bv[:, g * W:(g + 1) * W].unsqueeze(1).to_broadcast([P, 4, W]), ALU.add)
                    last.then_inc(v_ready, 1)

            def spread_q(no, ring):
                v.wait_ge(q_proj, no + 1)
                if not isinstance(no, int) or no >= 2:
                    v.wait_ge(s_ready, (no - 1) * HG)
                v.scalar_tensor_tensor(qbd[:, ring, :].rearrange("p (q h) -> p q h", h=HG),
                                       ps[:, Q_BANK, 0:P].unsqueeze(2).to_broadcast([P, P, HG]), bias[:, 0:1],
                                       qmask, ALU.add, ALU.mult).then_inc(q_ready, 1)

            def centre(no, k):
                sc = ps[:, S_BANK + k, 0:CPB * KEYS].rearrange("p (c n) -> p c n", n=KEYS)
                v.wait_ge(s_ready, no + 1)
                v.tensor_reduce(mx[:, k, :], sc, AX.X, ALU.max).then_inc(mx_ready, 1)
                if not isinstance(no, int) or no >= 2:
                    v.wait_ge(prob_ready, no - 1)
                v.wait_ge(mx_ready, no + 1)
                v.tensor_tensor(cen[:, k], sc, mx[:, k, :].unsqueeze(2).to_broadcast([P, CPB, KEYS]), ALU.subtract)\
                 .then_inc(cen_ready, 1)

            def residual(no):
                v.wait_ge(sel_ready, no + 1)
                xb = x[:, bass.ds(no, 1), :].rearrange("p a n -> p (a n)")
                v.tensor_tensor(xb, ps[:, PICK_BANK, PICK_AT:PICK_AT + D], xb, ALU.add).then_inc(x2_ready, 1)

            def attn_unit(b, blk, g, ring):
                no = blk + b * TILES
                inner = not isinstance(blk, int)
                centre(no * HG + g, g % 2)
                if g == 1 and (inner or blk >= 1):
                    weigh_half(no - 1, 1)
                if g == 2 and (inner or blk + 1 < TILES):
                    spread_q(no + 1, 1 - ring)
                if g == 3 and (inner or blk >= 1):
                    residual(no - 1)
                if g == 3:
                    weigh_half(no, 0)

            def weigh_half(no, z):
                o = ps[:, O_BANK + z, 0:HALF * VG].rearrange("p (a n) -> p a n", n=VG)
                v.wait_ge(o_ready, no * HG + 2 * (z + 1))
                v.reciprocal(rsum[:, z, :], o[:, :, W]).then_inc(rsum_ready, 1)
                v.wait_ge(rsum_ready, no * 2 + (z + 1))
                v.tensor_tensor(rmask[:, z], rsum[:, z, :].unsqueeze(2).to_broadcast([P, HALF, HG]),
                                const("dmask").unsqueeze(1).to_broadcast([P, HALF, HG]), ALU.mult).then_inc(rmask_ready, 1)
                if not isinstance(no, int) or no >= 1:
                    v.wait_ge(sel_ready, no)
                v.wait_ge(rmask_ready, no * 2 + (z + 1))
                v.tensor_tensor(omix[:, z].rearrange("p a (h d) -> p a h d", d=HD),
                                o[:, :, 0:W].rearrange("p a (h d) -> p a h d", d=HD),
                                rmask[:, z].unsqueeze(3).to_broadcast([P, HALF, HG, HD]), ALU.mult).then_inc(omix_ready, 1)

            def attn_blocks(b, lo, hi):
                with v.Fori(lo, hi - 1, 2) as blk:
                    for j in range(2):
                        for g in range(HG):
                            attn_unit(b, blk + j, g, (lo + j) % 2)

            def attn_block(b, blk):
                for g in range(HG):
                    attn_unit(b, blk, g, blk % 2)

            def attn_end(b):
                weigh_half(b * TILES + TILES - 1, 1)
                residual(b * TILES + TILES - 1)
                v.wait_ge(x2_ready, (b + 1) * TILES)

            v.wait_ge(x_arrived[0], 16)
            norm_stats(0)
            norm_var(0)
            norm_apply(R0B0, 0)
            v.wait_ge(const_in, 32)
            v.wait_ge(preset, 1)
            v.tensor_copy(tri_bf[:, :], const("tri")).then_inc(bf_ready, 1)
            v.tensor_copy(ones_bf[:, :], const("ones")).then_inc(bf_ready, 1)
            unit(0, 0)
            first_choice(0, SIDE_RUN)
            unit(0, 1)
            second_choice()
            unit(0, 2)
            gates(0, 0)
            unit(0, 3)
            expert_tiles(0, 0, SIDE_RUN)
            unit(0, 4)
            expert_rows(0, SIDE_RUN)
            v.wait_ge(x_arrived[1], 16)
            norm_stats(1)
            unit(0, 5)
            norm_var(1)
            unit(0, 6)
            norm_apply(R0B1, 1)
            unit(0, 7)
            unit(0, 8)
            first_choice(1, SIDE_RUN)
            unit(0, 9)
            second_choice()
            unit(0, 10)
            gates(1, 1)
            unit(0, 11)
            expert_tiles(1, 1, SIDE_RUN)
            unit(0, 12)
            expert_rows(1, SIDE_RUN)
            for i in range(13, 18):
                unit(0, i)
            routed_units(0, 18, 46)
            v.wait_ge(y_copied, B * TILES)
            for t in range(TILES):
                unit(0, 46 + t)
                combine(0, 0, t)
            unit(0, 54)
            norm_stats(0)
            unit(0, 55)
            norm_var(0)
            unit(0, 56)
            norm_apply(A_B0, 0)
            unit(0, 57)
            v.wait_ge(qkv_in, 16 * 5)
            v.tensor_scalar(bkg[:, :], const("gmask"), bias[:, 1:2], None, ALU.mult).then_inc(bkg_ready, 1)
            unit(0, 58)
            unit(0, 59)
            unit(0, 60)
            v.wait_ge(preset, 6)
            values(0, SIDE_RUN)
            unit(0, 61)
            drain(0)

            spread_q(0, 0)
            attn_block(0, 0)
            for blk in range(1, TILES - 2):
                for g in range(HG):
                    attn_unit(0, blk, g, blk % 2)
                    if g % 2 == 1 and blk * HG + g < 2 * TILES + 4:
                        combine(0, 1, (blk * HG + g - 5) // 2)
                    if (blk, g) == (5, 0):
                        norm_stats(1)
                    if (blk, g) == (5, 2):
                        norm_var(1)
            attn_unit(0, TILES - 2, 0, 0)
            norm_apply(A_B1, 1)
            for g in range(1, HG):
                attn_unit(0, TILES - 2, g, 0)
            v.wait_ge(v_stored, 16 * (V_PAD + 1))
            values(1, SIDE_ATTN)
            attn_block(0, TILES - 1)
            attn_end(0)

            spread_q(TILES, 0)
            attn_unit(1, 0, 0, 0)
            norm_stats(0)
            attn_unit(1, 0, 1, 0)
            norm_var(0)
            attn_unit(1, 0, 2, 0)
            norm_apply(R1B0, 0)
            attn_unit(1, 0, 3, 0)
            for g in range(HG):
                attn_unit(1, 1, g, 1)
                if g == 2:
                    first_choice(2, SIDE_ATTN)
                if g == 3:
                    second_choice()
            for g in range(HG):
                attn_unit(1, 2, g, 0)
                if g == 1:
                    gates(2, 0)
                if g == 2:
                    expert_tiles(2, 0, SIDE_ATTN)
                if g == 3:
                    expert_rows(0, SIDE_ATTN)
            attn_blocks(1, 3, TILES - 1)
            attn_block(1, TILES - 1)
            attn_end(1)

            copy_xt(1, routed_no(1, 0), 0)
            unit(1, 0)
            norm_stats(1)
            unit(1, 1)
            norm_var(1)
            unit(1, 2)
            norm_apply(R1B1, 1)
            unit(1, 3)
            unit(1, 4)
            first_choice(3, SIDE_RUN)
            unit(1, 5)
            second_choice()
            unit(1, 6)
            gates(3, 1)
            unit(1, 7)
            expert_tiles(3, 1, SIDE_RUN)
            unit(1, 8)
            expert_rows(1, SIDE_RUN)
            unit(1, 9)
            routed_units(1, 10, 30)
            for t in range(TILES):
                unit(1, 30 + t)
                combine(1, 0, t)
            routed_units(1, 38, 44)
            for i in range(44, 54):
                unit(1, i)
            for t in range(TILES):
                unit(1, 54 + t)
                combine(1, 1, t)
            drain(1)


def kernel(**inputs):
    import concourse.bacc as bacc
    from concourse.bass_utils import run_bass_kernel_spmd

    a = {k[3:]: np.asarray(v) for k, v in inputs.items()}
    up = np.concatenate([a["ffn_experts_w1"], a["ffn_shared_w1"][None]])
    down = np.concatenate([a["ffn_experts_w2"], a["ffn_shared_w2"][None]])
    arrays = {
        "x_in": a["attn_hidden_states"],
        "consts": shape_constants(),
        "w1t": up.transpose(2, 0, 1),
        "w2t": down.reshape(NEXP + 1, D, KCH, P).transpose(3, 0, 2, 1),
        "gate_wt": a["ffn_gate_w"].T,
        "wqt": a["attn_Wq"].T,
        "wkt": a["attn_Wk"].T,
        "wvt": a["attn_Wv"].T,
        "bqk": np.stack([a["attn_bq"], a["attn_bk"]], axis=1),
        "bv_rows": np.broadcast_to(a["attn_bv"], (P, D)),
    }
    arrays = {k: np.ascontiguousarray(v) for k, v in arrays.items()}
    nc = bacc.Bacc("TRN2", target_bir_lowering=False, num_devices=1)
    args = [nc.dram_tensor(k, v.shape, mybir.dt.from_np(v.dtype), kind="ExternalInput").ap() for k, v in arrays.items()]
    out = nc.dram_tensor("out", (B, S, D), mybir.dt.float32, kind="ExternalOutput").ap()
    macaron_kernel(nc, *args, out)
    r = run_bass_kernel_spmd(nc, [arrays], core_ids=[0])
    return r.results[0]["out"]
```

```python
import numpy as np
import concourse.bass as bass
from concourse import mybir
from contextlib import ExitStack

P = 128
B, S, D = 2, 1024, 128
HID, NEXP = 512, 8
SHARED = NEXP
TILES = S // P
KCH = HID // P
SLOT_TILES = (2 * S + NEXP * (P - 1)) // P
ROUTED = B * SLOT_TILES
UNITS = B * TILES + ROUTED
ROUTED0 = [B * TILES, 0]
SHARED0 = [0, ROUTED]
SHARED_BEFORE = [B * TILES, B * TILES]
HEADS, HD, W = 16, 8, 32
CHUNKS = S // W
CPB = P // W
HG = 4
KEYS = 3 * W
EPS = 1e-5
MASKED = -1.0e30

_WIDTHS = [("ident", P), ("tri", P), ("ones", P), ("sel", W), ("rep", P), ("beg", KEYS), ("end", KEYS),
           ("qmask", HG), ("gmask", HG), ("dmask", HG), ("rank", NEXP), ("cum", NEXP * NEXP), ("tile_no", SLOT_TILES),
           ("neg_half", TILES)]
CONST = {}
_at = 0
for _name, _w in _WIDTHS:
    CONST[_name] = (_at, _at + _w)
    _at += _w
NCONST = _at


def shape_constants():
    c = np.zeros((P, NCONST), np.float32)
    p = np.arange(P)

    def put(name, a):
        lo, hi = CONST[name]
        c[:, lo:hi] = np.asarray(a, np.float32).reshape(-1, hi - lo)

    put("ident", np.eye(P))
    put("tri", p[:, None] < p[None, :])
    put("ones", np.ones((P, P)))
    put("sel", (p[:, None] // HG) == np.arange(W)[None, :])
    put("rep", p[:, None] == (p[None, :] // HG))
    row, key = p[:, None] % W, np.arange(KEYS)[None, :]
    put("beg", np.where((key <= W) & (key < W - row), MASKED, 0.0))
    put("end", np.where((key >= 2 * W - 1) & (key - (2 * W - 1) >= W - row), MASKED, 0.0))
    inner = (p[:, None] % W) // HD == np.arange(HG)[None, :]
    put("qmask", inner * np.float32(1.0 / np.sqrt(HD)))
    put("gmask", p[:, None] // W == np.arange(HG)[None, :])
    put("dmask", p[:, None] % HG == np.arange(HG)[None, :])
    put("rank", np.tile(NEXP - np.arange(NEXP), (P, 1)))
    put("cum", np.tile((np.arange(NEXP)[None, :] <= np.arange(NEXP)[:, None]).ravel(), (P, 1)))
    put("tile_no", np.tile(np.arange(SLOT_TILES), (P, 1)))
    put("neg_half", np.full((P, TILES), -0.5))
    return c


def macaron_kernel(nc, x_in, consts, w1t, w2t, gate_wt, wqt, wkt, wvt, bqk, bv_rows, out):
    f32, bf16, i32 = mybir.dt.float32, mybir.dt.bfloat16, mybir.dt.int32
    ALU, ACT, AX = mybir.AluOpType, mybir.ActivationFunctionType, mybir.AxisListType

    ctx = ExitStack()
    with ctx:
        def sb(name, shape, dt=f32):
            return ctx.enter_context(nc.sbuf_tensor(name, shape, dt))

        def sem(name):
            return ctx.enter_context(nc.semaphore(name))

        rows = [nc.dram_tensor(f"expert_rows{b}", (SLOT_TILES * P, D), f32).ap() for b in range(B)]
        yrows = [nc.dram_tensor(f"expert_out{b}", (SLOT_TILES * P, D), f32).ap() for b in range(B)]
        vpad = [nc.dram_tensor(f"v_padded{b}", (S + 2 * W, D), f32).ap() for b in range(B)]

        cst = sb("cst", [P, NCONST])

        def const(name):
            lo, hi = CONST[name]
            return cst[:, lo:hi]

        ident, sel, rep = (const(n) for n in ("ident", "sel", "rep"))
        tri_bf, ones_bf = sb("tri_bf", [P, P], bf16), sb("ones_bf", [P, P], bf16)
        x = sb("x", [P, B * TILES, D])
        xn = sb("xn", [P, B * TILES, D])
        xnt = sb("xnt", [P, B * TILES, P])
        w1 = sb("w1", [P, NEXP + 1, HID])
        w2 = sb("w2", [P, NEXP + 1, KCH, D])
        gw = sb("gw", [P, NEXP])
        wq, wk, wv = sb("wq", [P, D]), sb("wk", [P, D]), sb("wv", [P, D])
        bias = sb("bias", [P, 2])
        bv = sb("bv", [P, D])
        zero = sb("zero", [P, D])

        stats = sb("stats", [P, B * TILES, 6])
        mv = sb("mv", [P, B * TILES, 2])
        vare = sb("vare", [P, B * TILES])
        rstd = sb("rstd", [P, B * TILES])

        logit = sb("logit", [P, TILES, NEXP])
        top = sb("top", [P, 2, TILES])
        hit = sb("hit", [P, TILES, NEXP])
        best = sb("best", [P, TILES])
        onehot = sb("onehot", [P, 2, TILES, NEXP])
        chosen = sb("chosen", [P, TILES + 1, NEXP], bf16)
        gap, egap = sb("gap", [P, TILES]), sb("egap", [P, TILES])
        rden = sb("rden", [P, TILES])
        gate = sb("gate", [P, B, 2, TILES])
        count = sb("count", [P, NEXP], i32)
        ntile = sb("ntile", [P, NEXP])
        ends8 = sb("ends8", [P, NEXP, NEXP])
        end_tile = sb("end_tile", [P, NEXP])
        base = sb("base", [P, NEXP])
        slot = sb("slot", [P, TILES, NEXP])
        slot2 = sb("slot2", [P, 2, TILES, NEXP])
        slotf = sb("slotf", [P, 2, TILES])
        slot_i = sb("slot_i", [P, B, 2, TILES], i32)
        passed = sb("passed", [1, SLOT_TILES, NEXP])
        tile_ef = sb("tile_ef", [1, SLOT_TILES])
        tile_e = sb("tile_e", [1, ROUTED], i32)

        xrow = sb("xrow", [P, 4, D])
        xt = sb("xt", [P, 2, P])
        th = sb("th", [P, 2, KCH * P])
        act = sb("act", [P, 2, KCH * P])
        w1u = sb("w1u", [P, 2, HID])
        yall = sb("yall", [P, ROUTED, D])
        got = sb("got", [P, 2, TILES, D])

        kt = sb("kt", [P, B, HG, S + 2 * W])
        bkg = sb("bkg", [P, HG])
        vsb = sb("vsb", [P, TILES, D])
        vwin = sb("vwin", [KEYS, B, CHUNKS, D])
        qbd = sb("qbd", [P, 2, P * HG])
        nmx = sb("nmx", [P, 2, CPB])
        prob = sb("prob", [P, 2, CPB, KEYS])
        prob_t = sb("prob_t", [KEYS, 2, CPB * P])
        sums = sb("sums", [P, 2, HG, CPB])
        sums_h = sb("sums_h", [P, HG, CPB, HG])
        omix = sb("omix", [P, CPB * P])
        rsum = sb("rsum", [P, 2, HEADS])
        att = sb("att", [P, D])

        ps = ctx.enter_context(nc.psum_tensor("ps", [P, 8, 512], f32))
        H_BANK = S_BANK = 0
        TURN_BANK, ROW_BANK, Y_BANK, O_BANK = 2, 3, 4, 4
        Q_BANK, PICK_BANK = 6, 7
        SIDE_RUN, SIDE_ATTN = (6, 7), (3, 3)

        def sems(names):
            return tuple(sem(n) for n in names.split())

        const_in, w_shared_in, w_in, qkv_in, zeroed, v_padded = sems("const_in w_shared_in w_in qkv_in zeroed v_padded")
        x0_arrived, x1_arrived = [sem(f"x0_arrived{h}") for h in range(2)], sem("x1_arrived")
        zero_set, preset, bf_ready, bkg_ready = sems("zero_set preset bf_ready bkg_ready")
        stats_ready = [sem(f"stats_ready{b}") for b in range(B)]
        vare_ready, rstd_ready, xc_ready, xn_ready, half_turned, half_copied = sems(
            "vare_ready rstd_ready xc_ready xn_ready half_turned half_copied")
        dve_step, logits_ready, chosen_ready, pos_ready = sems("dve_step logits_ready chosen_ready pos_ready")
        gap_ready, egap_ready, tiles_ready, route_ready = sems("gap_ready egap_ready tiles_ready route_ready")
        scattered = [sem(f"scattered{b}") for b in range(B)]
        row_in = [sem(f"row_in{i}") for i in range(4)]
        xt_turned, xt_ready, w1u_ready, h_ready, th_ready, act_ready, y_ready, y_copied = sems(
            "xt_turned xt_ready w1u_ready h_ready th_ready act_ready y_ready y_copied")
        y_stored = [sem(f"y_stored{b}") for b in range(B)]
        gathered = [sem(f"gathered{t}") for t in range(TILES)]
        added, combined, stored = sems("added combined stored")
        k_proj, k_ready, v_proj, v_ready, v_stored, vwin_in = sems("k_proj k_ready v_proj v_ready v_stored vwin_in")
        q_proj, q_ready, s_ready, mx_ready, prob_ready, sum_ready = sems("q_proj q_ready s_ready mx_ready prob_ready sum_ready")
        prob_turned, prob_t_ready, o_ready, omix_ready, mix_turned = sems("prob_turned prob_t_ready o_ready omix_ready mix_turned")
        sums_h_ready, sums_turned, rsum_ready, att_ready, x2_ready = sems("sums_h_ready sums_turned rsum_ready att_ready x2_ready")

        GROUPS = [(lo, min(lo + 4, SLOT_TILES)) for lo in range(0, SLOT_TILES, 4)]
        WARM_UP = 22
        V_PAD = 2 * B
        HALF = TILES // 2
        BLOCKS = B * TILES
        AU = BLOCKS * HG

        R0B0, R0B1, A_B0, A_B1, R1B0, R1B1 = range(6)
        NORM_OF_BATCH = [0, 0, 1, 1, 2, 2]

        def routed(r, i):
            return ROUTED0[r] <= i < ROUTED0[r] + ROUTED

        def unit_no(r, i):
            return r * UNITS + i

        def routed_no(r, i):
            return r * ROUTED + (i - ROUTED0[r])

        block = ctx.enter_context(nc.Block())

        @block.sync
        def _(sp):
            for h in range(2):
                sp.dma_start(x[:, h * HALF:(h + 1) * HALF],
                             x_in[0, h * HALF * P:(h + 1) * HALF * P].rearrange("(t p) d -> p t d", p=P)).then_inc(x0_arrived[h], 16)
            sp.dma_start(w1[:, SHARED], w1t[:, SHARED]).then_inc(w_shared_in, 16)
            sp.dma_start(w2[:, SHARED], w2t[:, SHARED]).then_inc(w_shared_in, 16)
            sp.dma_start(x[:, TILES:], x_in[1].rearrange("(t p) d -> p t d", p=P)).then_inc(x1_arrived, 16)
            sp.wait_ge(zero_set, 1)
            for b in range(B):
                sp.dma_start(rows[b].rearrange("(t p) d -> p t d", p=P),
                             zero[:, :].unsqueeze(1).to_broadcast([P, SLOT_TILES, D])).then_inc(zeroed, 16)
            sp.dma_start(w1[:, 0:NEXP], w1t[:, 0:NEXP]).then_inc(w_in, 16)
            sp.dma_start(w2[:, 0:NEXP], w2t[:, 0:NEXP]).then_inc(w_in, 16)
            for dst, src in ((wq, wqt), (wk, wkt), (wv, wvt), (bias, bqk), (bv, bv_rows)):
                sp.dma_start(dst[:, :], src).then_inc(qkv_in, 16)
            for b in range(B):
                for at in (0, S + W):
                    sp.dma_start(vpad[b][at:at + W, :], zero[0:W, :]).then_inc(v_padded, 16)

            def load_rows(r, b, lo, n):
                for j in range(n):
                    no = r * ROUTED + b * SLOT_TILES + lo + j
                    if not isinstance(lo, int) or no >= 4:
                        sp.wait_ge(xt_turned, no - 3)
                    k = no % 4 if isinstance(lo, int) else (r * ROUTED + b * SLOT_TILES + j) % 4
                    sp.dma_start(xrow[:, k], rows[b][bass.ds((lo + j) * P, P), :]).then_inc(row_in[k], 16)

            def store_y(r, b, lo, n):
                sp.wait_ge(y_copied, lo + (unit_no(r, ROUTED0[r]) + b * SLOT_TILES + n))
                sp.dma_start(yrows[b][bass.ds(lo * P, n * P), :].rearrange("(t p) d -> p t d", p=P),
                             yall[:, bass.ds(lo + b * SLOT_TILES, n), :]).then_inc(y_stored[b], 16)

            def last_stores(r, b, groups):
                for lo, hi in groups:
                    store_y(r, b, lo, hi - lo)

            def routed_tiles(r, b):
                sp.wait_ge(scattered[b], 16 * 2 * TILES * (r + 1))
                load_rows(r, b, 0, 3)
                if b:
                    last_stores(r, 0, GROUPS[4:5])
                load_rows(r, b, 3, 3)
                if b:
                    last_stores(r, 0, GROUPS[5:])
                load_rows(r, b, 6, 2)
                with sp.Fori(8, SLOT_TILES - 3 - 3, 4) as lo:
                    load_rows(r, b, lo, 4)
                    store_y(r, b, lo - 8, 4)
                load_rows(r, b, SLOT_TILES - 3, 3)
                last_stores(r, b, GROUPS[3:4])

            assert len(GROUPS) == 6
            routed_tiles(0, 0)
            routed_tiles(0, 1)
            last_stores(0, 1, GROUPS[4:])
            routed_tiles(1, 0)
            routed_tiles(1, 1)
            last_stores(1, 1, GROUPS[4:])
            pieces = [(0, 0, HALF), (0, HALF, HALF), (1, 0, HALF), (1, HALF, HALF - 1), (1, TILES - 1, 1)]
            for b, lo, n in pieces:
                sp.wait_ge(y_copied, unit_no(1, SHARED0[1]) + b * TILES + lo + n)
                sp.dma_start(out[b, lo * P:(lo + n) * P].rearrange("(t p) d -> p t d", p=P),
                             x[:, b * TILES + lo:b * TILES + lo + n]).then_inc(stored, 16)
            sp.wait_ge(stored, 16 * len(pieces))

        @block.gpsimd
        def _(pool):
            pool.memset(zero[:, :], 0.0).then_inc(zero_set, 1)
            pool.memset(chosen[:, TILES, :], 0.0).then_inc(preset, 1)

            def rstd_half(n, b, h):
                pool.wait_ge(vare_ready, 2 * n + h + 1)
                if n == 0 and h == 0:
                    pool.wait_ge(const_in, 32)
                ts = slice(b * TILES + h * HALF, b * TILES + (h + 1) * HALF)
                pool.tensor_tensor(rstd[:, ts], vare[:, ts], const("neg_half")[:, 0:HALF],
                                   ALU.pow).then_inc(rstd_ready, 1)

            centred = [0]

            def norm_half(n, b, h):
                rstd_half(n, b, h)
                pool.wait_ge(rstd_ready, 2 * n + h + 1)
                ts = slice(b * TILES + h * HALF, b * TILES + (h + 1) * HALF)
                pool.tensor_tensor(xn[:, ts, :], x[:, ts, :], mv[:, ts, 0:1].to_broadcast([P, HALF, D]),
                                   ALU.subtract).then_inc(xc_ready, 1)
                centred[0] += 1
                pool.wait_ge(xc_ready, centred[0])
                pool.tensor_tensor(xn[:, ts, :], xn[:, ts, :], rstd[:, ts].unsqueeze(2).to_broadcast([P, HALF, D]),
                                   ALU.mult).then_inc(xn_ready, 1)

            def scatter(f, b):
                pool.wait_ge(route_ready, f * B + b + 1)
                if f == 0:
                    pool.wait_ge(zeroed, 16 * B)
                for t in range(TILES):
                    for k in range(2):
                        pool.indirect_dma_start(
                            out=rows[b], out_offset=bass.IndirectOffsetOnAxis(ap=slot_i[:, b, k, t:t + 1], axis=0),
                            in_=xn[:, b * TILES + t, :], in_offset=None).then_inc(scattered[b], 16)

            def gather(f, b):
                if f * B + b:
                    pool.wait_ge(combined, (f * B + b) * TILES)
                pool.wait_ge(y_stored[b], 16 * len(GROUPS) * (f + 1))
                for t in range(TILES):
                    for k in range(2):
                        pool.indirect_dma_start(
                            out=got[:, k, t, :], out_offset=None, in_=yrows[b],
                            in_offset=bass.IndirectOffsetOnAxis(ap=slot_i[:, b, k, t:t + 1], axis=0)).then_inc(gathered[t], 16)

            def value_windows(b):
                pool.wait_ge(v_ready, 2 * (b + 1))
                pool.dma_start(vpad[b][W:W + S, :].rearrange("(t p) n -> p t n", p=P),
                             vsb[:, :, :]).then_inc(v_stored, 16)
                pool.wait_ge(v_padded, 16 * V_PAD)
                pool.wait_ge(v_stored, 16 * (b + 1))
                for part in range(3):
                    pool.dma_start(vwin[part * W:(part + 1) * W, b, :, :],
                                 vpad[b][part * W:part * W + S, :].rearrange("(c p) n -> p c n", p=W)).then_inc(vwin_in, 16)

            for h in range(2):
                rstd_half(R0B0, 0, h)
            pool.memset(kt[:, :, :, 0:W], 0.0).then_inc(preset, 1)
            pool.memset(kt[:, :, :, W + S:], 0.0).then_inc(preset, 1)
            for h in range(2):
                norm_half(R0B1, 1, h)
            scatter(0, 0)
            scatter(0, 1)
            gather(0, 0)
            for h in range(2):
                norm_half(A_B0, 0, h)
            value_windows(0)
            gather(0, 1)
            for h in range(2):
                norm_half(A_B1, 1, h)
            value_windows(1)
            norm_half(R1B0, 0, 0)
            rstd_half(R1B0, 0, 1)
            scatter(1, 0)
            norm_half(R1B1, 1, 0)
            rstd_half(R1B1, 1, 1)
            scatter(1, 1)
            gather(1, 0)
            gather(1, 1)

        @block.scalar
        def _(s):
            s.dma_start(cst[:, :], consts).then_inc(const_in, 16)
            s.dma_start(gw[:, :], gate_wt).then_inc(const_in, 16)
            def copy_half(n, b, h, banks):
                s.wait_ge(half_turned, 2 * n + h + 1)
                lo = b * TILES + 4 * h
                s.activation(xnt[:, lo:lo + 4, :].rearrange("p t n -> p (t n)"), ps[:, banks[h], :],
                             ACT.Copy).then_inc(half_copied, 1)

            def exp_gap(r):
                s.wait_ge(gap_ready, r + 1)
                s.activation(egap[:, :], gap[:, :], ACT.Exp).then_inc(egap_ready, 1)

            def keys(b, h, groups, banks):
                if b == 0 and h == 0:
                    s.wait_ge(preset, 3)
                    s.wait_ge(bkg_ready, 1)
                s.wait_ge(k_proj, 2 * b + h + 1)
                for g in groups:
                    s.activation(kt[:, b, g, W + h * 512:W + (h + 1) * 512], ps[:, banks[h], :], ACT.Identity,
                                 bias=bkg[:, g:g + 1], scale=const("gmask")[:, g:g + 1]).then_inc(k_ready, 1)

            def place_w1(r, i, k):
                e = s.value_load(tile_e[0:1, bass.ds(i - ROUTED0[r], 1)], min_val=0, max_val=NEXP - 1)
                no = i + routed_no(r, 0)
                if not isinstance(i, int) or no >= 2:
                    s.wait_ge(h_ready, no - 1 + SHARED_BEFORE[r])
                s.activation(w1u[:, k, :], w1[:, bass.ds(e, 1), :].rearrange("p a n -> p (a n)"),
                             ACT.Copy).then_inc(w1u_ready, 1)

            def tanh(no, k):
                s.wait_ge(h_ready, no + 1)
                if not isinstance(no, int) or no >= 2:
                    s.wait_ge(act_ready, no - 1)
                s.activation(th[:, k, :], ps[:, H_BANK + k, :], ACT.Tanh, scale=0.5).then_inc(th_ready, 1)

            def units(r, lo, hi):
                for i in range(lo, hi):
                    unit(r, i, i % 2)

            def unit(r, i, k):
                if not isinstance(i, int) or routed(r, i + 1) and i + 1 < UNITS:
                    place_w1(r, i + 1, 1 - k)
                tanh(i + unit_no(r, 0), k)

            def routed_units(r, lo, hi):
                assert routed(r, lo + 1) and routed(r, hi) and (hi - lo) % 2 == 0
                with s.Fori(lo, hi - 1, 2) as i:
                    for j in range(2):
                        unit(r, i + j, (lo + j) % 2)

            def exp(no, k):
                s.wait_ge(mx_ready, no + 1)
                if not isinstance(no, int) or no >= 2:
                    s.wait_ge(prob_turned, no - 1)
                    s.wait_ge(sum_ready, no - 1)
                for c in range(CPB):
                    last = s.activation(prob[:, k, c, :], ps[:, S_BANK + k, c * KEYS:(c + 1) * KEYS], ACT.Exp,
                                        bias=nmx[:, k, c:c + 1])
                last.then_inc(prob_ready, 1)

            def copy_prob(no, k):
                s.wait_ge(prob_turned, no + 1)
                if not isinstance(no, int) or no >= 2:
                    s.wait_ge(o_ready, no - 1)
                s.activation(prob_t[:, k, :], ps[0:KEYS, TURN_BANK, :], ACT.Copy).then_inc(prob_t_ready, 1)

            def attn_unit(v, k):
                if not isinstance(v, int) or v >= 2:
                    copy_prob(v - 2, k)
                if not isinstance(v, int) or v < AU:
                    exp(v, k)

            def attn(lo, hi):
                if lo >= 4 and hi - lo >= 6 and hi <= AU:
                    even = lo + (hi - lo) // 2 * 2
                    with s.Fori(lo, even - 1, 2) as v:
                        for j in range(2):
                            attn_unit(v + j, (lo + j) % 2)
                    lo = even
                for v in range(lo, hi):
                    attn_unit(v, v % 2)

            for h in range(2):
                copy_half(R0B0, 0, h, SIDE_RUN)
            units(0, 0, 2)
            exp_gap(0)
            units(0, 2, 5)
            for h in range(2):
                copy_half(R0B1, 1, h, SIDE_RUN)
            units(0, 5, 11)
            exp_gap(1)
            units(0, 11, 15)
            s.wait_ge(tiles_ready, 1)
            s.wait_ge(w_in, 16 * 2)
            units(0, 15, 18)
            routed_units(0, 18, 38)
            s.wait_ge(tiles_ready, 2)
            routed_units(0, 38, 54)
            units(0, 54, 55)
            copy_half(A_B0, 0, 0, SIDE_RUN)
            units(0, 55, 56)
            copy_half(A_B0, 0, 1, SIDE_RUN)
            units(0, 56, 58)
            for i in range(58, UNITS):
                units(0, i, i + 1)
                keys(0, (i - 58) // 2, ((0, 1), (2, 3))[i % 2], SIDE_RUN)
            attn(0, 4)
            attn(4, 17)
            copy_half(A_B1, 1, 0, SIDE_ATTN)
            attn(17, 22)
            copy_half(A_B1, 1, 1, SIDE_ATTN)
            attn(22, 26)
            keys(1, 0, (0, 1), SIDE_ATTN)
            attn(26, 27)
            keys(1, 0, (2, 3), SIDE_ATTN)
            attn(27, 29)
            keys(1, 1, (0, 1), SIDE_ATTN)
            attn(29, 30)
            keys(1, 1, (2, 3), SIDE_ATTN)
            attn(30, 34)
            copy_half(R1B0, 0, 0, SIDE_ATTN)
            attn(34, 42)
            copy_half(R1B0, 0, 1, SIDE_ATTN)
            attn(42, 50)
            exp_gap(2)
            attn(50, AU)
            s.wait_ge(tiles_ready, 3)
            place_w1(1, 0, 0)
            attn(AU, AU + 1)
            units(1, 0, 1)
            attn(AU + 1, AU + 2)
            units(1, 1, 3)
            copy_half(R1B1, 1, 0, SIDE_RUN)
            units(1, 3, 4)
            copy_half(R1B1, 1, 1, SIDE_RUN)
            units(1, 4, 10)
            exp_gap(3)
            routed_units(1, 10, 22)
            s.wait_ge(tiles_ready, 4)
            routed_units(1, 22, 44)
            units(1, 44, UNITS)

        @block.tensor
        def _(pe):
            def turn_half(n, b, h, banks):
                pe.wait_ge(xn_ready, 2 * n + h + 1)
                if h and banks[0] == banks[1]:
                    pe.wait_ge(half_copied, 2 * n + 1)
                for t in range(4):
                    last = pe.transpose(ps[:, banks[h], t * P:(t + 1) * P], xn[:, b * TILES + 4 * h + t, :], ident)
                last.then_inc(half_turned, 1)

            def logits(n, b, banks):
                for t in range(TILES):
                    if t % HALF == 0:
                        pe.wait_ge(half_copied, 2 * n + t // HALF + 1)
                    last = pe.matmul(ps[:, banks[0], t * NEXP:(t + 1) * NEXP], xnt[:, b * TILES + t, :], gw[:, :],
                                     start=True, stop=True)
                last.then_inc(logits_ready, 1)

            def ranks(r, banks):
                pe.wait_ge(chosen_ready, r + 1)
                for t in range(TILES):
                    pe.matmul(ps[:, banks[1], (t + 1) * NEXP:(TILES + 1) * NEXP].rearrange("p (t e) -> p t e", e=NEXP),
                              ones_bf[:, :], chosen[:, t:t + 1, :].to_broadcast([P, TILES - t, NEXP]),
                              start=(t == 0), stop=False, skip_group_check=True)
                pe.matmul(ps[:, banks[1], 0:(TILES + 1) * NEXP], tri_bf[:, :], chosen[:, :, :].rearrange("p t e -> p (t e)"),
                          start=False, stop=True, skip_group_check=True).then_inc(pos_ready, 1)

            def value_proj(n, b, h, banks):
                pe.wait_ge(half_copied, 2 * n + h + 1)
                if b == 0:
                    pe.wait_ge(qkv_in, 16 * 5)
                if h and banks[0] == banks[1]:
                    pe.wait_ge(v_ready, 2 * b + 1)
                for t in range(4):
                    last = pe.matmul(ps[:, banks[h], t * P:(t + 1) * P], xnt[:, b * TILES + 4 * h + t, :], wv[:, :],
                                     start=True, stop=True)
                last.then_inc(v_proj, 1)

            def key_proj(b, h, banks):
                pe.wait_ge(v_ready, 2 * b + (2 if banks[0] == banks[1] else h + 1))
                if h and banks[0] == banks[1]:
                    pe.wait_ge(k_ready, (2 * b + 1) * HG)
                lo = b * TILES + 4 * h
                pe.matmul(ps[:, banks[h], :], wk[:, :], xnt[:, lo:lo + 4, :].rearrange("p t n -> p (t n)"),
                          start=True, stop=True).then_inc(k_proj, 1)

            expert = {}

            def turn_rows(r, i):
                no = routed_no(r, i)
                pe.wait_ge(row_in[no % 4], 16 * (no // 4 + 1))
                if no >= 1:
                    pe.wait_ge(xt_ready, no)
                pe.transpose(ps[:, ROW_BANK, 0:P], xrow[:, no % 4, :], ident).then_inc(xt_turned, 1)
                x_at = i - ROUTED0[r]
                expert[i] = pe.value_load(tile_e[0:1, x_at:x_at + 1], min_val=0, max_val=NEXP - 1)

            def up(r, i):
                no = unit_no(r, i)
                if no >= 2:
                    pe.wait_ge(act_ready, no - 1)
                if routed(r, i):
                    pe.wait_ge(xt_ready, routed_no(r, i) + 1)
                    pe.wait_ge(w1u_ready, routed_no(r, i) + 1)
                    w, rows_t = w1u[:, routed_no(r, i) % 2, :], xt[:, routed_no(r, i) % 2, :]
                else:
                    w, rows_t = w1[:, SHARED, :], xnt[:, i - SHARED0[r], :]
                for c in range(KCH):
                    last = pe.matmul(ps[:, H_BANK + i % 2, c * P:(c + 1) * P], w[:, c * P:(c + 1) * P], rows_t,
                                     start=True, stop=True)
                last.then_inc(h_ready, 1)

            def down(r, i):
                no = unit_no(r, i)
                pe.wait_ge(act_ready, no + 1)
                if no >= 2:
                    pe.wait_ge(y_copied, no - 1)
                for c in range(KCH):
                    if routed(r, i):
                        w = w2[:, bass.ds(expert[i], 1), c, :].rearrange("p a n -> p (a n)")
                    else:
                        w = w2[:, SHARED, c, :]
                    last = pe.matmul(ps[:, Y_BANK + i % 2, 0:D], act[:, i % 2, c * P:(c + 1) * P], w,
                                     start=(c == 0), stop=(c == KCH - 1))
                last.then_inc(y_ready, 1)
                expert.pop(i, None)

            def units(r, lo, hi):
                for i in range(lo, hi):
                    if i < UNITS:
                        up(r, i)
                    if i + 1 < UNITS and routed(r, i + 1):
                        turn_rows(r, i + 1)
                    if i >= 1:
                        down(r, i - 1)

            def q_block(no):
                if no:
                    pe.wait_ge(q_ready, no)
                pe.matmul(ps[:, Q_BANK, 0:P], wq[:, :], xnt[:, no, :], start=True, stop=True).then_inc(q_proj, 1)

            def scores(v):
                blk, g = v // HG, v % HG
                b, t = blk // TILES, blk % TILES
                if g == 0:
                    pe.wait_ge(q_ready, blk + 1)
                if v >= 2:
                    pe.wait_ge(prob_ready, v - 1)
                for c in range(CPB):
                    mask = "beg" if t == 0 and c == 0 else "end" if t == TILES - 1 and c == CPB - 1 else None
                    dst = ps[:, S_BANK + v % 2, c * KEYS:(c + 1) * KEYS]
                    at = t * P + c * W
                    last = pe.matmul(dst, qbd[:, blk % 2, c * P:(c + 1) * P], kt[:, b, g, at:at + KEYS],
                                     start=True, stop=(mask is None))
                    if mask:
                        last = pe.matmul(dst, rep, const(mask), start=False, stop=True)
                last.then_inc(s_ready, 1)

            def turn_prob(v):
                pe.wait_ge(prob_ready, v + 1)
                if v >= 1:
                    pe.wait_ge(prob_t_ready, v)
                for c in range(CPB):
                    last = pe.transpose(ps[0:KEYS, TURN_BANK, c * P:(c + 1) * P], prob[:, v % 2, c, :], ident)
                last.then_inc(prob_turned, 1)

            def mix(v):
                blk, g = v // HG, v % HG
                b, t = blk // TILES, blk % TILES
                pe.wait_ge(prob_t_ready, v + 1)
                if g == 0 and blk >= 2:
                    pe.wait_ge(omix_ready, blk - 1)
                for c in range(CPB):
                    last = pe.matmul(ps[g * W:(g + 1) * W, O_BANK + blk % 2, c * P:(c + 1) * P],
                                     vwin[:, b, t * CPB + c, g * W:(g + 1) * W], prob_t[:, v % 2, c * P:(c + 1) * P],
                                     start=True, stop=True)
                last.then_inc(o_ready, 1)

            def block_sums(no):
                pe.wait_ge(sums_h_ready, no + 1)
                pe.wait_ge(q_ready, min(no + 2, BLOCKS))
                if no >= 1:
                    pe.wait_ge(rsum_ready, no)
                for c in range(CPB):
                    last = pe.matmul(ps[c * W:(c + 1) * W, Q_BANK, D:D + HEADS], sel, sums_h[:, :, c, :],
                                     start=True, stop=True)
                last.then_inc(sums_turned, 1)

            def turn_mix(no):
                pe.wait_ge(omix_ready, no + 1)
                if no >= 1:
                    pe.wait_ge(att_ready, no)
                heads = omix[:, :].rearrange("p (q h) -> p h q", h=HG)
                for h in range(HG):
                    at = h * (D - HD)
                    last = pe.transpose(ps[:, PICK_BANK, at:at + D], heads[:, h, :], ident)
                last.then_inc(mix_turned, 1)

            def attn(lo, hi):
                for v in range(lo, hi):
                    if v < AU:
                        scores(v)
                    if v % HG == 1 and v >= 2 * HG:
                        turn_mix(v // HG - 2)
                    if 2 <= v < AU + 2:
                        turn_prob(v - 2)
                    if v >= 3:
                        mix(v - 3)
                    if v % HG == 1:
                        if v >= HG:
                            block_sums(v // HG - 1)
                        if v // HG + 1 < BLOCKS:
                            q_block(v // HG + 1)

            pe.wait_ge(zero_set, 1)
            for _ in range(WARM_UP):
                pe.matmul(ps[:, H_BANK, 0:P], zero[:, :], zero[:, :], start=True, stop=True)
            pe.wait_ge(const_in, 32)
            for h in range(2):
                turn_half(R0B0, 0, h, SIDE_RUN)
            logits(R0B0, 0, SIDE_RUN)
            pe.wait_ge(w_shared_in, 16 * 2)
            units(0, 0, 2)
            pe.wait_ge(bf_ready, 2)
            ranks(0, SIDE_RUN)
            units(0, 2, 4)
            for h in range(2):
                turn_half(R0B1, 1, h, SIDE_RUN)
            units(0, 4, 6)
            logits(R0B1, 1, SIDE_RUN)
            units(0, 6, 12)
            ranks(1, SIDE_RUN)
            units(0, 12, ROUTED0[0] - 1)
            pe.wait_ge(tiles_ready, 1)
            pe.wait_ge(w_in, 16 * 2)
            units(0, ROUTED0[0] - 1, ROUTED0[0] + SLOT_TILES - 1)
            pe.wait_ge(tiles_ready, 2)
            units(0, ROUTED0[0] + SLOT_TILES - 1, 54)
            turn_half(A_B0, 0, 0, SIDE_RUN)
            units(0, 54, 56)
            turn_half(A_B0, 0, 1, SIDE_RUN)
            value_proj(A_B0, 0, 0, SIDE_RUN)
            units(0, 56, 57)
            value_proj(A_B0, 0, 1, SIDE_RUN)
            units(0, 57, 59)
            for h in range(2):
                key_proj(0, h, SIDE_RUN)
            units(0, 59, 61)
            pe.wait_ge(k_ready, HG)
            q_block(0)
            units(0, 61, UNITS)
            pe.wait_ge(act_ready, UNITS - 1)
            attn(0, 1)
            units(0, UNITS, UNITS + 1)
            pe.wait_ge(act_ready, UNITS)
            attn(1, 3)
            pe.wait_ge(vwin_in, 16 * 3)
            pe.wait_ge(y_copied, UNITS)
            attn(3, 17)
            turn_half(A_B1, 1, 0, SIDE_ATTN)
            attn(17, 19)
            value_proj(A_B1, 1, 0, SIDE_ATTN)
            attn(19, 22)
            pe.wait_ge(v_ready, 3)
            turn_half(A_B1, 1, 1, SIDE_ATTN)
            attn(22, 24)
            value_proj(A_B1, 1, 1, SIDE_ATTN)
            attn(24, 26)
            key_proj(1, 0, SIDE_ATTN)
            attn(26, 29)
            key_proj(1, 1, SIDE_ATTN)
            attn(29, 32)
            pe.wait_ge(k_ready, 4 * HG)
            attn(32, 34)
            turn_half(R1B0, 0, 0, SIDE_ATTN)
            attn(34, 35)
            pe.wait_ge(vwin_in, 16 * 3 * 2)
            attn(35, 42)
            turn_half(R1B0, 0, 1, SIDE_ATTN)
            attn(42, 44)
            logits(R1B0, 0, SIDE_ATTN)
            attn(44, 50)
            ranks(2, SIDE_ATTN)
            attn(50, AU)
            pe.wait_ge(tiles_ready, 3)
            pe.wait_ge(route_ready, 3)
            turn_rows(1, 0)
            attn(AU, AU + 1)
            pe.wait_ge(prob_ready, AU)
            units(1, 0, 1)
            attn(AU + 1, AU + 3)
            up(1, 1)
            turn_rows(1, 2)
            turn_mix(BLOCKS - 1)
            down(1, 0)
            units(1, 2, 3)
            pe.wait_ge(att_ready, BLOCKS)
            turn_half(R1B1, 1, 0, SIDE_RUN)
            units(1, 3, 4)
            turn_half(R1B1, 1, 1, SIDE_RUN)
            units(1, 4, 5)
            logits(R1B1, 1, SIDE_RUN)
            units(1, 5, 9)
            ranks(3, SIDE_RUN)
            units(1, 9, SLOT_TILES - 1)
            pe.wait_ge(tiles_ready, 4)
            units(1, SLOT_TILES - 1, UNITS + 1)

        @block.vector
        def _(v):
            steps = [0]

            def step(ins):
                steps[0] += 1
                ins.then_inc(dve_step, 1)
                v.wait_ge(dve_step, steps[0])

            def tile_stats(tile):
                b = tile // TILES
                v.bn_stats(stats[:, tile, :], x[:, tile, :]).then_inc(stats_ready[b], 1)

            def norm_var(n, b, h):
                v.wait_ge(stats_ready[b], TILES * NORM_OF_BATCH[n] + HALF * (h + 1))
                ts = slice(b * TILES + h * HALF, b * TILES + (h + 1) * HALF)
                for t in range(ts.start, ts.stop):
                    last = v.bn_aggr(mv[:, t, :], stats[:, t, :])
                step(last)
                v.tensor_scalar(vare[:, ts], mv[:, ts, 1], EPS, None, ALU.add).then_inc(vare_ready, 1)

            def norm_apply(n, b, h):
                v.wait_ge(rstd_ready, 2 * n + h + 1)
                for t in range(b * TILES + h * HALF, b * TILES + (h + 1) * HALF):
                    last = v.tensor_scalar(xn[:, t, :], x[:, t, :], mv[:, t, 0:1], rstd[:, t:t + 1],
                                           ALU.subtract, ALU.mult)
                last.then_inc(xn_ready, 1)

            def over_experts(a):
                return a.unsqueeze(2).to_broadcast([P, TILES, NEXP])

            rank = const("rank").unsqueeze(1).to_broadcast([P, TILES, NEXP])

            def top_logit(k):
                step(v.tensor_reduce(top[:, k, :], logit[:, :, :], AX.X, ALU.max))
                step(v.tensor_tensor(hit[:, :, :], logit[:, :, :], over_experts(top[:, k, :]), ALU.is_equal))

            def first_with_it(k):
                step(v.tensor_tensor(hit[:, :, :], hit[:, :, :], rank, ALU.mult))
                step(v.tensor_reduce(best[:, :], hit[:, :, :], AX.X, ALU.max))
                step(v.tensor_tensor(onehot[:, k], rank, over_experts(best[:, :]), ALU.is_equal))

            def first_logit(r, banks):
                v.wait_ge(logits_ready, r + 1)
                step(v.tensor_copy(logit[:, :, :], ps[:, banks[0], 0:TILES * NEXP].rearrange("p (t e) -> p t e", e=NEXP)))
                top_logit(0)

            def second_logit():
                step(v.scalar_tensor_tensor(logit[:, :, :], onehot[:, 0], -3.0e38, logit[:, :, :], ALU.mult, ALU.add))
                top_logit(1)

            def both_choices():
                first_with_it(1)
                v.tensor_tensor(chosen[:, 0:TILES, :], onehot[:, 0], onehot[:, 1], ALU.add).then_inc(chosen_ready, 1)
                v.tensor_tensor(gap[:, :], top[:, 1, :], top[:, 0, :], ALU.subtract).then_inc(gap_ready, 1)

            def gates(r, b):
                v.wait_ge(egap_ready, r + 1)
                step(v.tensor_scalar(rden[:, :], egap[:, :], 1.0, None, ALU.add))
                step(v.reciprocal(rden[:, :], rden[:, :]))
                step(v.tensor_scalar(gate[:, b, 0, :], rden[:, :], 0.25, None, ALU.mult))
                step(v.tensor_tensor(gate[:, b, 1, :], gate[:, b, 0, :], egap[:, :], ALU.mult))

            def expert_ends(r, banks):
                v.wait_ge(pos_ready, r + 1)
                step(v.tensor_scalar(count[:, :], ps[:, banks[1], TILES * NEXP:(TILES + 1) * NEXP], float(P - 1), None,
                                     ALU.add))
                step(v.tensor_scalar(count[:, :], count[:, :], P.bit_length() - 1, None, ALU.logical_shift_right))
                step(v.tensor_copy(ntile[:, :], count[:, :]))
                step(v.tensor_tensor(ends8[:, :, :], ntile[:, :].unsqueeze(1).to_broadcast([P, NEXP, NEXP]),
                                     const("cum").rearrange("p (a c) -> p a c", c=NEXP), ALU.mult))
                step(v.tensor_reduce(end_tile[:, :], ends8[:, :, :], AX.X, ALU.add))

            def tile_experts(b):
                step(v.tensor_tensor(passed[:, :, :], end_tile[0:1, :].unsqueeze(1).to_broadcast([1, SLOT_TILES, NEXP]),
                                     const("tile_no")[0:1, :].unsqueeze(2).to_broadcast([1, SLOT_TILES, NEXP]), ALU.is_le))
                step(v.tensor_reduce(tile_ef[:, :], passed[:, :, :], AX.X, ALU.add))
                v.tensor_scalar(tile_e[:, b * SLOT_TILES:(b + 1) * SLOT_TILES], tile_ef[:, :], float(NEXP - 1), None,
                                ALU.min).then_inc(tiles_ready, 1)

            def rank_slots(banks):
                pos = ps[:, banks[1], 0:TILES * NEXP].rearrange("p (t e) -> p t e", e=NEXP)
                step(v.tensor_tensor(base[:, :], end_tile[:, :], ntile[:, :], ALU.subtract))
                step(v.tensor_scalar(base[:, :], base[:, :], float(P), None, ALU.mult))
                step(v.tensor_tensor(slot[:, :, :], pos, base[:, :].unsqueeze(1).to_broadcast([P, TILES, NEXP]), ALU.add))

            def token_rows(b):
                v.tensor_tensor(slot2[:, 0], slot[:, :, :], onehot[:, 0], ALU.mult)
                step(v.tensor_tensor(slot2[:, 1], slot[:, :, :], onehot[:, 1], ALU.mult))
                step(v.tensor_reduce(slotf[:, :, :], slot2[:, :, :, :], AX.X, ALU.add))
                v.tensor_copy(slot_i[:, b, :, :], slotf[:, :, :]).then_inc(route_ready, 1)

            def add_expert(f, b, t, k):
                no = (f * B + b) * TILES + t
                xs = x[:, b * TILES + t, :]
                if k == 0:
                    v.wait_ge(gathered[t], 16 * 2 * (f * B + b + 1))
                else:
                    v.wait_ge(added, no + 1)
                v.scalar_tensor_tensor(xs, got[:, k, t, :], gate[:, b, k, t:t + 1], xs, ALU.mult, ALU.add)\
                 .then_inc((added, combined)[k], 1)

            def combine(f, b, t):
                if t < TILES:
                    add_expert(f, b, t, 0)
                if t >= 1:
                    add_expert(f, b, t - 1, 1)
                if t >= 2 and f == 0:
                    combined_stats(b, t - 2)
                if t == TILES and f == 0:
                    combined_stats(b, t - 1)

            def combined_stats(b, t):
                v.wait_ge(combined, b * TILES + t + 1)
                tile_stats(b * TILES + t)

            def copy_xt(r, no, k):
                v.wait_ge(xt_turned, no + 1)
                if not isinstance(no, int) or no >= 2:
                    v.wait_ge(h_ready, no - 1 + SHARED_BEFORE[r])
                v.tensor_copy(xt[:, k, :], ps[:, ROW_BANK, 0:P]).then_inc(xt_ready, 1)

            def silu(no, k):
                v.wait_ge(th_ready, no + 1)
                if not isinstance(no, int) or no >= 2:
                    v.wait_ge(y_ready, no - 1)
                v.scalar_tensor_tensor(act[:, k, :], th[:, k, :], 1.0, ps[:, H_BANK + k, :], ALU.add,
                                       ALU.mult).then_inc(act_ready, 1)

            def take_y(r, i, k, is_routed):
                v.wait_ge(y_ready, i + (unit_no(r, 0) + 1))
                y = ps[:, Y_BANK + k, 0:D]
                if is_routed:
                    at = i - ROUTED0[r]
                    v.tensor_copy(yall[:, bass.ds(at, 1), :].rearrange("p a n -> p (a n)"), y).then_inc(y_copied, 1)
                else:
                    xs = x[:, i - SHARED0[r], :]
                    if r == 1:
                        v.wait_ge(combined, (2 * B - 1) * TILES + max(0, i - SHARED0[1] - TILES + 1))
                    v.scalar_tensor_tensor(xs, y, 0.25, xs, ALU.mult, ALU.add).then_inc(y_copied, 1)

            def unit(r, i):
                if i + 1 < UNITS and routed(r, i + 1):
                    copy_xt(r, routed_no(r, i + 1), (i + 1) % 2)
                silu(unit_no(r, i), i % 2)
                if i >= 1:
                    take_y(r, i - 1, (i - 1) % 2, routed(r, i - 1))

            def routed_units(r, lo, hi):
                assert (hi - lo) % 2 == 0 and routed(r, lo - 1) and routed(r, hi)
                with v.Fori(lo, hi - 1, 2) as i:
                    for j in range(2):
                        k = (lo + j) % 2
                        copy_xt(r, i + (routed_no(r, 0) + j + 1), 1 - k)
                        silu(i + (unit_no(r, 0) + j), k)
                        take_y(r, i + (j - 1), 1 - k, True)

            def drain(r):
                for i in range(UNITS - 1, UNITS):
                    take_y(r, i, i % 2, routed(r, i))

            qmask = const("qmask").unsqueeze(1).to_broadcast([P, P, HG])

            def values(b, h, banks):
                v.wait_ge(v_proj, 2 * b + h + 1)
                v.tensor_tensor(vsb[:, 4 * h:4 * h + 4, :], ps[:, banks[h], :].rearrange("p (t n) -> p t n", n=D),
                                bv[:, :].unsqueeze(1).to_broadcast([P, 4, D]), ALU.add).then_inc(v_ready, 1)

            def spread_q(no, ring):
                v.wait_ge(q_proj, no + 1)
                if no >= 2:
                    v.wait_ge(s_ready, (no - 1) * HG)
                v.scalar_tensor_tensor(qbd[:, ring, :].rearrange("p (q h) -> p q h", h=HG),
                                       ps[:, Q_BANK, 0:P].unsqueeze(2).to_broadcast([P, P, HG]), bias[:, 0:1],
                                       qmask, ALU.add, ALU.mult).then_inc(q_ready, 1)

            def maxima(no, k):
                v.wait_ge(s_ready, no + 1)
                if no >= 2:
                    v.wait_ge(prob_ready, no - 1)
                sc = ps[:, S_BANK + k, 0:CPB * KEYS].rearrange("p (c n) -> p c n", n=KEYS)
                v.tensor_reduce(nmx[:, k, :], sc, AX.X, ALU.max, negate=True).then_inc(mx_ready, 1)

            def sum_probs(no, k, ring, g):
                v.wait_ge(prob_ready, no + 1)
                v.tensor_reduce(sums[:, ring, g, :], prob[:, k], AX.X, ALU.add).then_inc(sum_ready, 1)

            def spread_sums(no, ring):
                v.wait_ge(sum_ready, (no + 1) * HG)
                if no >= 1:
                    v.wait_ge(sums_turned, no)
                v.tensor_tensor(sums_h[:, :, :, :].rearrange("p g c h -> p (g c) h"),
                                sums[:, ring, :, :].rearrange("p g c -> p (g c)").unsqueeze(2).to_broadcast([P, HG * CPB, HG]),
                                const("dmask").unsqueeze(1).to_broadcast([P, HG * CPB, HG]), ALU.mult).then_inc(sums_h_ready, 1)

            def copy_mix(no, ring):
                v.wait_ge(o_ready, (no + 1) * HG)
                if no >= 1:
                    v.wait_ge(mix_turned, no)
                v.tensor_copy(omix[:, :], ps[:, O_BANK + ring, :]).then_inc(omix_ready, 1)

            def invert_sums(no, ring):
                v.wait_ge(sums_turned, no + 1)
                v.reciprocal(rsum[:, ring, :], ps[:, Q_BANK, D:D + HEADS]).then_inc(rsum_ready, 1)

            def residual(no, ring):
                v.wait_ge(mix_turned, no + 1)
                v.wait_ge(rsum_ready, no + 1)
                own = ps[:, PICK_BANK, 0:HG * D].rearrange("p (h g k d) -> p h g k d", h=HG, g=HG, d=HD)[:, :, :, 0, :]
                v.tensor_tensor(att[:, :].rearrange("p (g h d) -> p h g d", h=HG, d=HD), own,
                                rsum[:, ring, :].rearrange("p (g h) -> p h g", h=HG).unsqueeze(3)
                                .to_broadcast([P, HG, HG, HD]), ALU.mult).then_inc(att_ready, 1)
                v.wait_ge(att_ready, no + 1)
                v.tensor_tensor(x[:, no, :], att[:, :], x[:, no, :], ALU.add).then_inc(x2_ready, 1)

            def residual_stats(no, b):
                v.wait_ge(x2_ready, no + 1)
                v.bn_stats(stats[:, no, :], x[:, no, :]).then_inc(stats_ready[b], 1)

            def attn_unit(u):
                blk, g, ring = u // HG, u % HG, u // HG % 2
                if u < AU:
                    maxima(u, g % 2)
                if 0 < u <= AU:
                    sum_probs(u - 1, 1 - g % 2, ring if g else 1 - ring, (g - 1) % HG)
                if g == 0 and 1 <= blk <= BLOCKS:
                    spread_sums(blk - 1, 1 - ring)
                if g == 1 and blk + 1 < BLOCKS:
                    spread_q(blk + 1, 1 - ring)
                if g == 2 and 1 <= blk <= BLOCKS:
                    invert_sums(blk - 1, 1 - ring)
                if g == 2 and blk >= 2:
                    residual(blk - 2, ring)
                if g == 3 and blk >= 2:
                    residual_stats(blk - 2, (blk - 2) // TILES)
                if g == 3 and 1 <= blk <= BLOCKS:
                    copy_mix(blk - 1, 1 - ring)

            def attn(lo, hi):
                for u in range(lo, hi):
                    attn_unit(u)

            for h in range(2):
                v.wait_ge(x0_arrived[h], 16)
                for t in range(h * HALF, (h + 1) * HALF):
                    tile_stats(t)
                norm_var(R0B0, 0, h)
            for h in range(2):
                norm_apply(R0B0, 0, h)
            v.wait_ge(x1_arrived, 16)
            for t in range(TILES, 2 * TILES):
                tile_stats(t)
            for h in range(2):
                norm_var(R0B1, 1, h)
            v.wait_ge(const_in, 32)
            v.wait_ge(preset, 1)
            v.tensor_copy(tri_bf[:, :], const("tri")).then_inc(bf_ready, 1)
            v.tensor_copy(ones_bf[:, :], const("ones")).then_inc(bf_ready, 1)
            first_logit(0, SIDE_RUN)
            first_with_it(0)
            unit(0, 0)
            second_logit()
            both_choices()
            unit(0, 1)
            expert_ends(0, SIDE_RUN)
            rank_slots(SIDE_RUN)
            token_rows(0)
            unit(0, 2)
            tile_experts(0)
            unit(0, 3)
            gates(0, 0)
            for i in range(4, 7):
                unit(0, i)
            first_logit(1, SIDE_RUN)
            unit(0, 7)
            first_with_it(0)
            unit(0, 8)
            second_logit()
            unit(0, 9)
            both_choices()
            unit(0, 10)
            unit(0, 11)
            gates(1, 1)
            unit(0, 12)
            expert_ends(1, SIDE_RUN)
            unit(0, 13)
            rank_slots(SIDE_RUN)
            unit(0, 14)
            tile_experts(1)
            unit(0, 15)
            token_rows(1)
            unit(0, 16)
            unit(0, 17)
            routed_units(0, 18, 44)
            v.wait_ge(y_copied, B * TILES)
            for t in range(TILES + 1):
                unit(0, 44 + t)
                combine(0, 0, t)
                if t == HALF + 1:
                    norm_var(A_B0, 0, 0)
            norm_var(A_B0, 0, 1)
            unit(0, 53)
            v.wait_ge(qkv_in, 16 * 5)
            v.tensor_scalar(bkg[:, :], const("gmask"), bias[:, 1:2], None, ALU.mult).then_inc(bkg_ready, 1)
            for i in range(54, 57):
                unit(0, i)
            values(0, 0, SIDE_RUN)
            unit(0, 57)
            values(0, 1, SIDE_RUN)
            for i in range(58, 61):
                unit(0, i)
            spread_q(0, 0)
            unit(0, 61)
            drain(0)

            attn(0, 5)
            for t in range(TILES + 1):
                attn(5 + 3 * t // 2, 5 + 3 * (t + 1) // 2)
                combine(0, 1, t)
                if t == HALF + 1:
                    norm_var(A_B1, 1, 0)
            norm_var(A_B1, 1, 1)
            attn(5 + 3 * (TILES + 1) // 2, 19)
            v.wait_ge(v_stored, 16)
            values(1, 0, SIDE_ATTN)
            attn(19, 24)
            values(1, 1, SIDE_ATTN)
            attn(24, 28)
            norm_var(R1B0, 0, 0)
            attn(28, 40)
            norm_var(R1B0, 0, 1)
            attn(40, 41)
            norm_apply(R1B0, 0, 1)
            attn(41, 45)
            first_logit(2, SIDE_ATTN)
            attn(45, 46)
            first_with_it(0)
            attn(46, 47)
            second_logit()
            attn(47, 48)
            both_choices()
            attn(48, 51)
            expert_ends(2, SIDE_ATTN)
            attn(51, 52)
            rank_slots(SIDE_ATTN)
            attn(52, 53)
            token_rows(0)
            attn(53, 54)
            tile_experts(0)
            gates(2, 0)
            attn(54, 56)
            norm_var(R1B1, 1, 0)
            attn(56, AU)
            copy_xt(1, routed_no(1, 0), 0)
            attn(AU, AU + 2)
            unit(1, 0)
            attn(AU + 2, AU + 4)
            residual(BLOCKS - 1, (BLOCKS - 1) % 2)
            residual_stats(BLOCKS - 1, 1)

            norm_var(R1B1, 1, 1)
            unit(1, 1)
            norm_apply(R1B1, 1, 1)
            for i in range(2, 6):
                unit(1, i)
            first_logit(3, SIDE_RUN)
            first_with_it(0)
            unit(1, 6)
            second_logit()
            unit(1, 7)
            both_choices()
            unit(1, 8)
            unit(1, 9)
            expert_ends(3, SIDE_RUN)
            unit(1, 10)
            rank_slots(SIDE_RUN)
            token_rows(1)
            unit(1, 11)
            tile_experts(1)
            unit(1, 12)
            gates(3, 1)
            unit(1, 13)
            routed_units(1, 14, 30)
            for t in range(TILES + 1):
                unit(1, 30 + t)
                combine(1, 0, t)
            unit(1, 39)
            routed_units(1, 40, 44)
            for i in range(44, 53):
                unit(1, i)
            for t in range(TILES + 1):
                unit(1, 53 + t)
                combine(1, 1, t)
            drain(1)


def kernel(**inputs):
    import concourse.bacc as bacc
    from concourse.bass_utils import run_bass_kernel_spmd

    a = {k[3:]: np.asarray(v) for k, v in inputs.items()}
    up = np.concatenate([a["ffn_experts_w1"], a["ffn_shared_w1"][None]])
    down = np.concatenate([a["ffn_experts_w2"], a["ffn_shared_w2"][None]])
    arrays = {
        "x_in": a["attn_hidden_states"],
        "consts": shape_constants(),
        "w1t": up.transpose(2, 0, 1),
        "w2t": down.reshape(NEXP + 1, D, KCH, P).transpose(3, 0, 2, 1),
        "gate_wt": a["ffn_gate_w"].T,
        "wqt": a["attn_Wq"].T,
        "wkt": a["attn_Wk"].T,
        "wvt": a["attn_Wv"].T,
        "bqk": np.stack([a["attn_bq"], a["attn_bk"]], axis=1),
        "bv_rows": np.broadcast_to(a["attn_bv"], (P, D)),
    }
    arrays = {k: np.ascontiguousarray(v) for k, v in arrays.items()}
    nc = bacc.Bacc("TRN2", target_bir_lowering=False, num_devices=1)
    args = [nc.dram_tensor(k, v.shape, mybir.dt.from_np(v.dtype), kind="ExternalInput").ap() for k, v in arrays.items()]
    out = nc.dram_tensor("out", (B, S, D), mybir.dt.float32, kind="ExternalOutput").ap()
    macaron_kernel(nc, *args, out)
    r = run_bass_kernel_spmd(nc, [arrays], core_ids=[0])
    return r.results[0]["out"]
```
